# Optimizing a Trainium2 kernel written in Bass

```python
import numpy as np
import jax
import jax.numpy as jnp

def _softmax(x, axis=-1):
    return jax.nn.softmax(x, axis=axis)

def _gelu(x):
    return jax.nn.gelu(x, approximate=True)

def _silu(x):
    return jax.nn.silu(x)

def _sigmoid(x):
    return jax.nn.sigmoid(x)

def _layernorm(x, axis=-1, eps=1e-05):
    m = jnp.mean(x, axis=axis, keepdims=True)
    v = jnp.var(x, axis=axis, keepdims=True)
    return (x - m) / jnp.sqrt(v + eps)

def _scatter_add(tgt, idx, src, axis=0):
    return tgt.at[idx].add(src)

def _segment_sum(src, seg, n):
    return jax.ops.segment_sum(src, seg, n)
kernel_name = 'mk_adj_seq_d2_adj_r2_fcadf4'

def setup_inputs(seed: int=0):
    np.random.seed(seed)
    _w = jnp.asarray

    def _rec_inputs():
        import jax
        import jax.numpy as jnp
        _gk = jax.random.key(seed)
        x = -0.0005207 + 1.001 * jax.random.normal(jax.random.fold_in(_gk, 1), (128, 128, 256), jnp.float32)
        _a = jax.random.bernoulli(jax.random.fold_in(_gk, 2), 0.03125, (128, 128, 128))
        _a = jnp.logical_or(_a, jnp.swapaxes(_a, -1, -2))
        _a = jnp.logical_or(_a, jnp.eye(128, dtype=bool))
        adj = _a.astype(jnp.int32)
        return (x, adj)
    x, adj = _rec_inputs()

    def _L0_gnn_setup():
        import jax, jax.numpy as jnp
        import numpy as np
        B, S, D, H = (2, 1024, 256, 8)
        HD = D // H
        EPS = 1e-05

        def _ln(x, g, b):
            mu = jnp.mean(x, axis=-1, keepdims=True)
            var = jnp.mean((x - mu) ** 2, axis=-1, keepdims=True)
            return (x - mu) * jax.lax.rsqrt(var + EPS) * g + b
        key = jax.random.key(seed)
        ks = jax.random.split(key, 16)
        x = jax.random.normal(ks[0], (B, S, D), dtype=jnp.float32)
        adj = jax.random.randint(ks[1], (B, S, S), 0, 2, dtype=jnp.int32)
        adj = adj.at[:, jnp.arange(S), jnp.arange(S)].set(1)
        edge_attr = jax.random.normal(ks[2], (B, S, S), dtype=jnp.float32)
        sc = 1.0 / np.sqrt(D)
        p = lambda k, shp: jax.random.normal(k, shp, dtype=jnp.float32) * sc
        return {'x': x, 'adj_matrix': adj, 'edge_attr_matrix': edge_attr, 'ln1_g': jnp.ones((D,)), 'ln1_b': jnp.zeros((D,)), 'ln2_g': jnp.ones((D,)), 'ln2_b': jnp.zeros((D,)), 'wq': p(ks[3], (D, D)), 'bq': jnp.zeros((D,)), 'wk': p(ks[4], (D, D)), 'bk': jnp.zeros((D,)), 'wv': p(ks[5], (D, D)), 'bv': jnp.zeros((D,)), 'wo': p(ks[6], (D, D)), 'bo': jnp.zeros((D,)), 'w1': p(ks[7], (D, 4 * D)), 'b1': jnp.zeros((4 * D,)), 'w2': p(ks[8], (4 * D, D)), 'b2': jnp.zeros((D,))}
    _L0_gnn_all = _L0_gnn_setup()
    _L0_gnn_in = {k: v for k, v in _L0_gnn_all.items() if k in ('ln1_g', 'ln1_b', 'ln2_g', 'ln2_b', 'wq', 'bq', 'wk', 'bk', 'wv', 'bv', 'wo', 'bo', 'w1', 'b1', 'w2', 'b2')}
    del _L0_gnn_all

    def _L1_gnn_setup():
        import jax, jax.numpy as jnp
        import numpy as np
        B, N, E, FF, L = (8, 1024, 256, 128, 2)
        LN_EPS = 1e-05
        SCALE = float(np.sqrt(FF))

        def layer_norm(x, g, b):
            m = jnp.mean(x, axis=-1, keepdims=True)
            v = jnp.mean(jnp.square(x - m), axis=-1, keepdims=True)
            return (x - m) * jax.lax.rsqrt(v + LN_EPS) * g + b
        key = jax.random.key(seed)
        ks = jax.random.split(key, 9)
        s = 0.02
        node_fts = jax.random.normal(ks[0], (B, N, E), jnp.float32)
        rel_edges = jax.random.randint(ks[1], (B, N, N), 0, 2, jnp.int32)
        Wq = jax.random.normal(ks[2], (L, FF, E), jnp.float32) * s
        bq = jnp.zeros((L, FF), jnp.float32)
        Wk = jax.random.normal(ks[3], (L, FF, E), jnp.float32) * s
        bk = jnp.zeros((L, FF), jnp.float32)
        Wc = jax.random.normal(ks[4], (L, E, E), jnp.float32) * s
        ln_g = jnp.ones((L, E), jnp.float32)
        ln_b = jnp.zeros((L, E), jnp.float32)
        return {'node_fts': node_fts, 'rel_edges': rel_edges, 'Wq': Wq, 'bq': bq, 'Wk': Wk, 'bk': bk, 'Wc': Wc, 'ln_g': ln_g, 'ln_b': ln_b}
    _L1_gnn_all = _L1_gnn_setup()
    _L1_gnn_in = {k: v for k, v in _L1_gnn_all.items() if k in ('Wq', 'bq', 'Wk', 'bk', 'Wc', 'ln_g', 'ln_b')}
    del _L1_gnn_all
    return {'x': x, 'adj': adj, 'L0_gnn_ln1_g': _L0_gnn_in['ln1_g'], 'L0_gnn_ln1_b': _L0_gnn_in['ln1_b'], 'L0_gnn_ln2_g': _L0_gnn_in['ln2_g'], 'L0_gnn_ln2_b': _L0_gnn_in['ln2_b'], 'L0_gnn_wq': _L0_gnn_in['wq'], 'L0_gnn_bq': _L0_gnn_in['bq'], 'L0_gnn_wk': _L0_gnn_in['wk'], 'L0_gnn_bk': _L0_gnn_in['bk'], 'L0_gnn_wv': _L0_gnn_in['wv'], 'L0_gnn_bv': _L0_gnn_in['bv'], 'L0_gnn_wo': _L0_gnn_in['wo'], 'L0_gnn_bo': _L0_gnn_in['bo'], 'L0_gnn_w1': _L0_gnn_in['w1'], 'L0_gnn_b1': _L0_gnn_in['b1'], 'L0_gnn_w2': _L0_gnn_in['w2'], 'L0_gnn_b2': _L0_gnn_in['b2'], 'L1_gnn_Wq': _L1_gnn_in['Wq'], 'L1_gnn_bq': _L1_gnn_in['bq'], 'L1_gnn_Wk': _L1_gnn_in['Wk'], 'L1_gnn_bk': _L1_gnn_in['bk'], 'L1_gnn_Wc': _L1_gnn_in['Wc'], 'L1_gnn_ln_g': _L1_gnn_in['ln_g'], 'L1_gnn_ln_b': _L1_gnn_in['ln_b']}

def reference(x, adj, L0_gnn_ln1_g, L0_gnn_ln1_b, L0_gnn_ln2_g, L0_gnn_ln2_b, L0_gnn_wq, L0_gnn_bq, L0_gnn_wk, L0_gnn_bk, L0_gnn_wv, L0_gnn_bv, L0_gnn_wo, L0_gnn_bo, L0_gnn_w1, L0_gnn_b1, L0_gnn_w2, L0_gnn_b2, L1_gnn_Wq, L1_gnn_bq, L1_gnn_Wk, L1_gnn_bk, L1_gnn_Wc, L1_gnn_ln_g, L1_gnn_ln_b):
    import jax
    import jax.numpy as jnp

    def _L0_gnn_ref(x, adj_matrix, edge_attr_matrix, ln1_g, ln1_b, ln2_g, ln2_b, wq, bq, wk, bk, wv, bv, wo, bo, w1, b1, w2, b2):
        import jax, jax.numpy as jnp
        import numpy as np
        B, S, D, H = (2, 1024, 256, 8)
        HD = D // H
        EPS = 1e-05

        def _ln(x, g, b):
            mu = jnp.mean(x, axis=-1, keepdims=True)
            var = jnp.mean((x - mu) ** 2, axis=-1, keepdims=True)
            return (x - mu) * jax.lax.rsqrt(var + EPS) * g + b
        b, s, d = x.shape
        residual = x
        nx = _ln(x, ln1_g, ln1_b)
        q = (nx @ wq + bq).reshape(b, s, H, HD).transpose(0, 2, 1, 3)
        k = (nx @ wk + bk).reshape(b, s, H, HD).transpose(0, 2, 1, 3)
        v = (nx @ wv + bv).reshape(b, s, H, HD).transpose(0, 2, 1, 3)
        adjf = adj_matrix.astype(jnp.float32)
        bias = jnp.where(adj_matrix > 0, 0.1 * edge_attr_matrix * adjf, -jnp.inf)[:, None]
        scores = jnp.einsum('bhqd,bhkd->bhqk', q, k) / np.sqrt(HD) + bias
        attn = jax.nn.softmax(scores, axis=-1)
        out = jnp.einsum('bhqk,bhkd->bhqd', attn, v)
        out = out.transpose(0, 2, 1, 3).reshape(b, s, d)
        x1 = residual + (out @ wo + bo)
        n2 = _ln(x1, ln2_g, ln2_b)
        mlp = jax.nn.gelu(n2 @ w1 + b1, approximate=False) @ w2 + b2
        return x1 + mlp

    def _L1_gnn_ref(node_fts, rel_edges, Wq, bq, Wk, bk, Wc, ln_g, ln_b):
        import jax, jax.numpy as jnp
        import numpy as np
        B, N, E, FF, L = (8, 1024, 256, 128, 2)
        LN_EPS = 1e-05
        SCALE = float(np.sqrt(FF))

        def layer_norm(x, g, b):
            m = jnp.mean(x, axis=-1, keepdims=True)
            v = jnp.mean(jnp.square(x - m), axis=-1, keepdims=True)
            return (x - m) * jax.lax.rsqrt(v + LN_EPS) * g + b
        x = node_fts
        mask = rel_edges == 0
        for k in range(L):
            q = jnp.einsum('bnd,fd->bnf', x, Wq[k]) + bq[k]
            kk = jnp.einsum('bnd,fd->bnf', x, Wk[k]) + bk[k]
            scores = jnp.einsum('bof,bif->boi', q, kk) / SCALE
            scores = jnp.where(mask, -10000000000.0, scores)
            attn = jax.nn.softmax(scores, axis=2)
            attn = jnp.where(mask, 0.0, attn)
            ctx = jnp.einsum('boi,bid->bod', attn, x)
            ctx = jnp.einsum('bnd,ed->bne', ctx, Wc[k])
            x = layer_norm(x + ctx, ln_g[k], ln_b[k])
        return x
    x = _L0_gnn_ref(x, adj, adj, L0_gnn_ln1_g, L0_gnn_ln1_b, L0_gnn_ln2_g, L0_gnn_ln2_b, L0_gnn_wq, L0_gnn_bq, L0_gnn_wk, L0_gnn_bk, L0_gnn_wv, L0_gnn_bv, L0_gnn_wo, L0_gnn_bo, L0_gnn_w1, L0_gnn_b1, L0_gnn_w2, L0_gnn_b2)
    x = _L1_gnn_ref(x, adj, L1_gnn_Wq, L1_gnn_bq, L1_gnn_Wk, L1_gnn_bk, L1_gnn_Wc, L1_gnn_ln_g, L1_gnn_ln_b)
    return x

_drawn_inputs = setup_inputs


def setup_inputs(seed=0):
    import zlib

    import numpy as np

    out = dict(_drawn_inputs(seed))
    spreads = {'L0_gnn_ln1_g': (1.0, 0.2),
     'L0_gnn_ln1_b': (0.0, 0.1),
     'L0_gnn_ln2_g': (1.0, 0.2),
     'L0_gnn_ln2_b': (0.0, 0.1),
     'L0_gnn_bq': (0.0, 0.1),
     'L0_gnn_bk': (0.0, 0.8),
     'L0_gnn_bv': (0.0, 0.1),
     'L0_gnn_bo': (0.0, 0.1),
     'L0_gnn_b1': (0.0, 0.1),
     'L0_gnn_b2': (0.0, 0.1),
     'L1_gnn_bq': (0.0, 0.8),
     'L1_gnn_bk': (0.0, 0.8),
     'L1_gnn_ln_g': (1.0, 0.2),
     'L1_gnn_ln_b': (0.0, 0.1)}
    factors = {}
    for name, (base, spread) in spreads.items():
        noise = np.random.default_rng([zlib.crc32(name.encode()), seed]).standard_normal(out[name].shape)
        drawn = base * np.exp(spread * noise) if base else spread * noise
        out[name] = jnp.asarray(drawn.astype(out[name].dtype))
    for name, factor in factors.items():
        out[name] = (out[name] * factor).astype(out[name].dtype)
    return out
```

```python
import math
from contextlib import ExitStack

import concourse.bass as bass
from concourse import mybir

F32, F32R, F16, I32 = (mybir.dt.float32, mybir.dt.float32r, mybir.dt.float16, mybir.dt.int32)
ALU, ACT, AX = mybir.AluOpType, mybir.ActivationFunctionType, mybir.AxisListType

P = 128
D = 256
KC = D // P
H, HD = 8, 32
FF = 4 * D
FC = FF // P
B = 4
R = B * P
L = 2
VW = HD + 2
EPS = 1e-5
MASKED = -1e30
P_SCALE = math.log(1024.0)
RING = 4

ORDER = [
    "C0.xT", "A.q0", "A.q1", "C0.q", "C0.k", "A.k0", "C0.S", "A.k1", "M.xT", "C0.xW", "A.v0",
    "M.up0", "C0.PT", "M.up1", "C0.PV", "M.up2", "A.v1", "M.up3", "M.up4", "M.down0", "M.up5",
    "M.down1", "M.up6", "M.down2", "M.up7", "M.down3",
    "A.S0", "C1.xT", "M.down4", "A.S1", "C1.q", "C1.k", "A.PT0", "C1.S", "A.S2", "M.down5",
    "A.AV0", "A.PT1", "C1.xW", "A.S3", "A.AV1", "A.PT2", "C1.PT", "M.down6", "A.AV2", "A.PT3",
    "C1.PV", "A.AV3", "A0.xT", "A.oT", "M.down7", "A.wo",
]


def graph_blocks(nc, x, adj, ln1_g, ln1_b, ln2_g, ln2_b, wq, bq, wk, bk, wv, bv, wo, bo, w1, b1,
                 w2, b2, cWq, cbq, cbk, cWk, cWc, c_g, c_b, out):
    NG = x.shape[0] // B
    x_dram = x.rearrange("(g t b) p d -> g t p b d", t=2, b=B)
    adj_dram = adj.rearrange("(g t b) p k -> g t p b k", t=2, b=B)
    out_dram = out.rearrange("(g t b) p d -> g t p b d", t=2, b=B)

    with ExitStack() as ctx:
        def sb(name, shape, dt=F32):
            return ctx.enter_context(nc.sbuf_tensor(name, shape, dt))

        def sem(name):
            return ctx.enter_context(nc.semaphore(name))

        ident = sb("ident", [P, P])
        wqk_h, wqk_l = sb("wqk_h", [P, KC, 2 * D], F32R), sb("wqk_l", [P, KC, 2 * D], F32R)
        wv_h, wv_l = sb("wv_h", [P, KC, D], F32R), sb("wv_l", [P, KC, D], F32R)
        wo_h, wo_l = sb("wo_h", [P, KC, D], F32R), sb("wo_l", [P, KC, D], F32R)
        w1_h, w1_l = sb("w1_h", [P, KC, FF], F32R), sb("w1_l", [P, KC, FF], F32R)
        w2_h, w2_l = sb("w2_h", [P, FC, D], F32R), sb("w2_l", [P, FC, D], F32R)
        cqk_h, cqk_l = sb("cqk_h", [P, L, KC, 2 * P], F32R), sb("cqk_l", [P, L, KC, 2 * P], F32R)
        cw_h, cw_l = sb("cw_h", [P, L, KC, D], F32R), sb("cw_l", [P, L, KC, D], F32R)
        ln_col = sb("ln_col", [P, 4, KC])
        bqk_col = sb("bqk_col", [P, 4])
        bv_col = sb("bv_col", [P, KC])
        b1_col = sb("b1_col", [P, FC])
        cb_col = sb("cb_col", [P, 2, L])
        ln_q = sb("ln_q", [P, KC])
        bv_rep = sb("bv_rep", [P, KC, P])
        bo_row, b2_row = sb("bo_row", [P, D]), sb("b2_row", [P, D])
        cg_row, cb_row = sb("cg_row", [P, L, D]), sb("cb_row", [P, L, D])
        minus_half, eps_cols = sb("minus_half", [P, B]), sb("eps_cols", [P, B])

        area = sb("area", [P, 8192])
        sc = area[:, 0:2048].rearrange("p (s h k) -> p s h k", s=2, h=H)
        hidden = area[:, 0:1024].rearrange("p (s n) -> p s n", s=2)
        o_rows = area[:, 2048:3072].rearrange("p (b d) -> p b d", b=B)
        x1 = o_rows
        x1b = area[:, 3072:4096].rearrange("p (b d) -> p b d", b=B)
        x2 = area[:, 4096:5120].rearrange("p (b d) -> p b d", b=B)
        cW = area[:, 5120:6144].rearrange("p (b d) -> p b d", b=B)
        cy = area[:, 6144:7168].rearrange("p (b d) -> p b d", b=B)
        cs = area[:, 7168:7680].rearrange("p (b k) -> p b k", b=B)
        cPT = area[:, 7680:8192].rearrange("p (b k) -> p b k", b=B)
        raw_qkvo = area[:, 0:2048].rearrange("p (w c n) -> p w c n", w=4, c=KC)
        raw_w1 = area[:, 2048:4096].rearrange("p (c n) -> p c n", c=KC)
        raw_w2 = area[:, 4096:6144].rearrange("p (c n) -> p c n", c=FC)
        raw_cqk = area[:, 6144:7168].rearrange("p (l w n) -> p l w n", l=L, w=2)
        raw_cw = area[:, 7168:8192].rearrange("p (l c n) -> p l c n", l=L, c=KC)

        xin = sb("xin", [P, 2, B, D])
        xhat = sb("xhat", [P, B, D])
        xT_h, xT_l = sb("xT_h", [P, KC, R], F32R), sb("xT_l", [P, KC, R], F32R)
        half = sb("half", [P, 4096], F16)
        qk16 = half[:, :].rearrange("p (s t n) -> p s t n", s=2, t=4)
        pT16 = half[:, :].rearrange("p (u s h q) -> p u s h q", u=2, s=2, h=H)
        qS, kS = sb("qS", [P, 2, 4, R], F16), sb("kS", [P, 2, 4, R], F16)
        v_h, v_l = sb("v_h", [P, B, H, VW], F16), sb("v_l", [P, B, H, VW], F16)
        rot_h, rot_l = sb("rot_h", [P, KC, R], F32R), sb("rot_l", [P, KC, R], F32R)
        hid_h, hid_l = sb("hid_h", [P, RING, R], F32R), sb("hid_l", [P, RING, R], F32R)
        cT_h, cT_l = sb("cT_h", [P, KC, R], F32R), sb("cT_l", [P, KC, R], F32R)
        cq, ck = sb("cq", [P, R]), sb("ck", [P, R])
        adjA, adjC = sb("adjA", [P, B, P], I32), sb("adjC", [P, B, P], I32)
        biasA, biasC = sb("biasA", [P, B, P]), sb("biasC", [P, B, P])
        mtmp = sb("mtmp", [P, B, P])
        nmax = sb("nmax", [P, B, H])
        nbias = sb("nbias", [P, B, H])
        rec = sb("rec", [P, B, H])
        st1, st2, st3 = (sb(f"st{n}", [P, B, 6]) for n in (1, 2, 3))
        mv1, mv2, mv3 = (sb(f"mv{n}", [P, B, 2]) for n in (1, 2, 3))
        ve1, ve2, ve3 = (sb(f"ve{n}", [P, B]) for n in (1, 2, 3))
        rs1, rs2, rs3 = (sb(f"rs{n}", [P, B]) for n in (1, 2, 3))
        cmax, csum, crec, cscale = (sb(n, [P, B]) for n in ("cmax", "csum", "crec", "cscale"))

        ps = ctx.enter_context(nc.psum_tensor("ps", [P, 8, 512], F32))
        psA, psA1 = ps[:, 0:2, :], ps[:, 2, :]
        psUp = (ps[:, 3, :], ps[:, 2, :])
        psM = ps[:, 4:6, :]
        psC = ps[:, 6:8, :]
        psA_rows = psA.rearrange("p c (b d) -> p (c b) d", d=D)
        psM_rows = psM.rearrange("p c (b d) -> p (c b) d", d=D)
        psC_rows = psC.rearrange("p c (b d) -> p (c b) d", d=D)
        psA_heads = psA.rearrange("p c (h k) -> p (c h) k", k=P)
        psC_S = ps[:, 6, :].rearrange("p (b k) -> p b k", b=B)
        psC_PT = ps[:, 7, :].rearrange("p (b k) -> p b k", b=B)
        psAV = ps[:, 2, 0:H * VW].rearrange("p (h c) -> p h c", h=H)

        ld_raw = [sem(f"ld_raw{n}") for n in range(4)]
        ld_vec = sem("ld_vec")
        const_ok = sem("const_ok")
        prep_pe = sem("prep_pe")
        prep_dve = sem("prep_dve")
        ld_x = [sem(f"ld_x{n}") for n in range(2)]
        ld_adjA, ld_adjC = sem("ld_adjA"), sem("ld_adjC")
        st_out = sem("st_out")
        stk = sem("stk")
        STK = 24 * 16
        waited = sem("waited")
        t_xT, t_qk, t_v, t_S = sem("t_xT"), sem("t_qk"), sem("t_v"), sem("t_S")
        t_PT, t_AV, t_oT, t_wo = sem("t_PT"), sem("t_AV"), sem("t_oT"), sem("t_wo")
        t_mT, t_up, t_down = sem("t_mT"), sem("t_up"), sem("t_down")
        t_cT, t_cqk, t_cW, t_cS = sem("t_cT"), sem("t_cqk"), sem("t_cW"), sem("t_cS")
        t_cPT, t_cPV = sem("t_cPT"), sem("t_cPV")
        a_xT, a_qk, a_v, a_exp = sem("a_xT"), sem("a_qk"), sem("a_v"), sem("a_exp")
        a_PT, a_oT, a_mT, a_gelu = sem("a_PT"), sem("a_oT"), sem("a_mT"), sem("a_gelu")
        a_cT, a_cqk, a_cW = sem("a_cT"), sem("a_cqk"), sem("a_cW")
        a_cexp, a_cPT = sem("a_cexp"), sem("a_cPT")
        d_st1, d_mv1, d_xT, d_qk, d_v = (sem("d_" + n) for n in ("st1", "mv1", "xT", "qk", "v"))
        d_mt, d_mA, d_mC = sem("d_mt"), sem("d_mA"), sem("d_mC")
        d_S, d_max, d_nb = sem("d_S"), sem("d_max"), sem("d_nb")
        d_PT, d_rec, d_o, d_oT, d_x1 = (sem("d_" + n) for n in ("PT", "rec", "o", "oT", "x1"))
        d_st2, d_mv2, d_mT, d_lo, d_x2 = (sem("d_" + n) for n in ("st2", "mv2", "mT", "lo", "x2"))
        d_cT, d_cS, d_cmax, d_cnb = (sem("d_" + n) for n in ("cT", "cS", "cmax", "cnb"))
        d_hi = sem("d_hi")
        d_crec, d_csc, d_cy, d_cst, d_cmv = (sem("d_" + n) for n in ("crec", "csc", "cy", "cst", "cmv"))
        p_ve1, p_rs1, p_x1, p_xb = (sem("p_" + n) for n in ("ve1", "rs1", "x1", "xb"))
        p_ve2, p_rs2, p_x2, p_x1b = (sem("p_" + n) for n in ("ve2", "rs2", "x2", "x1b"))
        p_ve3, p_rs3, p_xc, p_cg, p_c = (sem("p_" + n) for n in ("ve3", "rs3", "xc", "cg", "c"))

        def need(eng, signal, g, per, k):
            if g is None:
                return
            pair, odd = g
            if isinstance(pair, int):
                count = (2 * pair + odd) * per + k
                if count > 0:
                    eng.wait_ge(signal, count)
            else:
                eng.wait_ge(signal, pair * (2 * per) + (odd * per + k))

        def apart(eng):
            eng.sem_inc(waited, 1)

        def mm3(pe, dst, lh, ll, rh, rl, start, stop, **kw):
            pe.matmul(dst, lh, rh, start=start, stop=False, **kw)
            pe.matmul(dst, lh, rl, start=False, stop=False, **kw)
            return pe.matmul(dst, ll, rh, start=False, stop=stop, **kw)

        def groups(it, odd):
            def group(back):
                par = (odd - back) % 2
                pair = it + (odd - back - par) // 2
                if isinstance(it, int) and not 0 <= 2 * pair + par < NG:
                    return None
                return pair, par
            return group(-1), group(0), group(1), group(2)

        def run(eng, iteration):
            iteration(-1, 1)
            iteration(0, 0)
            iteration(0, 1)
            with eng.Fori(1, NG // 2 - 1) as it:
                iteration(it, 0)
                iteration(it, 1)
            for n in range(NG - 2, NG + 2):
                iteration(n // 2, n % 2)

        PREP_DVE = 8 + 2 * (3 * KC + 1 + KC + 3 * L + 1)
        NVEC = 12 + 2 * L
        block = ctx.enter_context(nc.Block())

        @block.sync
        def _(sp):
            for n, v in enumerate((ln1_g, ln1_b, ln2_g, ln2_b)):
                sp.dma_start(ln_col[:, n, :], v.rearrange("(c p) -> p c", p=P),
                             allow_slow_non_contiguous=True).then_inc(ld_vec, 16)
            sp.dma_start(bqk_col[:, 0:2], bq.rearrange("(c p) -> p c", p=P),
                             allow_slow_non_contiguous=True).then_inc(ld_vec, 16)
            sp.dma_start(bqk_col[:, 2:4], bk.rearrange("(c p) -> p c", p=P),
                             allow_slow_non_contiguous=True).then_inc(ld_vec, 16)
            sp.dma_start(bv_col[:, :], bv.rearrange("(c p) -> p c", p=P),
                             allow_slow_non_contiguous=True).then_inc(ld_vec, 16)
            sp.dma_start(b1_col[:, :], b1.rearrange("(c p) -> p c", p=P),
                             allow_slow_non_contiguous=True).then_inc(ld_vec, 16)
            sp.dma_start(cb_col[:, 0, :], cbq.rearrange("l p -> p l"),
                             allow_slow_non_contiguous=True).then_inc(ld_vec, 16)
            sp.dma_start(cb_col[:, 1, :], cbk.rearrange("l p -> p l"),
                             allow_slow_non_contiguous=True).then_inc(ld_vec, 16)
            sp.dma_start(bo_row[:, :], bo.partition_broadcast(P)).then_inc(ld_vec, 16)
            sp.dma_start(b2_row[:, :], b2.partition_broadcast(P)).then_inc(ld_vec, 16)
            for l in range(L):
                sp.dma_start(cg_row[:, l, :], c_g[l].partition_broadcast(P)).then_inc(ld_vec, 16)
                sp.dma_start(cb_row[:, l, :], c_b[l].partition_broadcast(P)).then_inc(ld_vec, 16)
            sp.dma_start(xin[:, 0], x_dram[0, 0]).then_inc(ld_x[0], 16)
            for n, w in enumerate((wq, wk, wv, wo)):
                sp.dma_start(raw_qkvo[:, n], w.rearrange("(c p) n -> p c n", p=P)).then_inc(ld_raw[0], 16)
            sp.dma_start(raw_w1, w1.rearrange("(c p) n -> p c n", p=P)).then_inc(ld_raw[1], 16)
            for l in range(L):
                sp.dma_start(raw_cqk[:, l, 0], cWq[l]).then_inc(ld_raw[3], 16)
                sp.dma_start(raw_cqk[:, l, 1], cWk[l]).then_inc(ld_raw[3], 16)
                sp.dma_start(raw_cw[:, l], cWc[l].rearrange("(c p) n -> p c n", p=P)).then_inc(ld_raw[3], 16)
            sp.dma_start(raw_w2, w2.rearrange("(c p) n -> p c n", p=P)).then_inc(ld_raw[2], 16)
            sp.dma_start(adjA[:, :, :], adj_dram[0, 0]).then_inc(ld_adjA, 16)

            def rows(dram, g):
                return dram[bass.ds(g[0], 1), g[1]].rearrange("o p b d -> p (o b) d")

            def iteration(it, odd):
                g0, gA, gM, gC = groups(it, odd)
                g_next = groups(it + 1, odd)[1]
                for w, (stack, parts) in enumerate(((qS, (0, 0, 1)), (kS, (0, 1, 0)))):
                    if gA is not None:
                        need(sp, a_qk, gA, 4, 2 * w + 2)
                        need(sp, d_qk, gA, 4, 2 * w + 2)
                        need(sp, t_S, gA, 4, 0)
                        for slot, part in enumerate(parts):
                            for j in range(4):
                                sp.dma_start(stack[32 * slot:32 * slot + 32, :, j, :],
                                             qk16[32 * j:32 * j + 32, part, 2 * w:2 * w + 2, :])\
                                  .then_inc(stk, 16)
                if gM is not None:
                    need(sp, d_mC, gM, 1, 0)
                    apart(sp)
                    sp.dma_start(adjC[:, :, :], rows(adj_dram, gM)).then_inc(ld_adjC, 16)
                if g0 is not None and gA is not None:
                    need(sp, d_mA, g0, 1, 0)
                    apart(sp)
                    sp.dma_start(adjA[:, :, :], rows(adj_dram, g0)).then_inc(ld_adjA, 16)
                if g_next is not None:
                    need(sp, d_x1, g_next, 1, -1)
                    apart(sp)
                    sp.dma_start(xin[:, g_next[1]], rows(x_dram, g_next)).then_inc(ld_x[g_next[1]], 16)
                if gC is not None:
                    need(sp, p_c, gC, 2, 2)
                    apart(sp)
                    sp.dma_start(rows(out_dram, gC), cy).then_inc(st_out, 16)

            run(sp, iteration)
            sp.wait_ge(st_out, 16 * NG)

        @block.gpsimd
        def _(pool):
            pool.memset(ident[:, :], 0.0).then_inc(const_ok, 1)
            pool.memset(minus_half[:, :], -0.5).then_inc(const_ok, 1)
            pool.memset(eps_cols[:, :], EPS).then_inc(const_ok, 1)
            pool.memset(v_h[:, :, :, HD:VW], 1.0).then_inc(const_ok, 1)
            pool.memset(v_l[:, :, :, HD:VW], 0.0).then_inc(const_ok, 1)
            pool.wait_ge(const_ok, 5)
            pool.affine_select(out=ident[:, :], in_=ident[:, :], compare_op=ALU.not_equal, fill=1.0,
                               base=0, pattern=[[-1, P]], channel_multiplier=1).then_inc(const_ok, 1)
            pool.wait_ge(const_ok, 6)

            def rsqrt(g, per, k, mv, ve, rs, ve_ok, rs_ok):
                pool.tensor_tensor(ve[:, :], mv[:, :, 1], eps_cols[:, :], ALU.add).then_inc(ve_ok, 1)
                need(pool, ve_ok, g, per, k)
                pool.tensor_tensor(rs[:, :], ve[:, :], minus_half[:, :], ALU.pow).then_inc(rs_ok, 1)
                need(pool, rs_ok, g, per, k)

            def norm(dst, src, mv, rs):
                apart(pool)
                for b in range(B):
                    last = pool.tensor_scalar(dst[:, b, :], src[:, b, :], mv[:, b, 0:1], rs[:, b:b + 1],
                                              ALU.subtract, ALU.mult)
                return last

            def over_graphs(row):
                return row.unsqueeze(1).broadcast_to([P, B, D])

            def iteration(it, odd):
                g0, gA, gM, gC = groups(it, odd)
                for step in ORDER:
                    if step == "M.down3" and g0 is not None:
                        need(pool, d_mv1, g0, B, B)
                        rsqrt(g0, 1, 1, mv1, ve1, rs1, p_ve1, p_rs1)
                        need(pool, t_xT, g0, 1, 0)
                        need(pool, t_mT, gM, 1, 1)
                        norm(xhat, xin[:, g0[1]], mv1, rs1).then_inc(p_x1, 1)
                        need(pool, p_x1, g0, 1, 1)
                        pool.wait_ge(prep_dve, PREP_DVE)
                        pool.tensor_tensor(xin[:, g0[1]], xin[:, g0[1]], over_graphs(bo_row[:, :]),
                                           ALU.add).then_inc(p_xb, 1)
                    if step in ("C0.PV", "C1.PV") and gC is not None:
                        l = int(step[1])
                        need(pool, d_cmv, gC, 2 * B, B * l + B)
                        rsqrt(gC, 2, l + 1, mv3, ve3, rs3, p_ve3, p_rs3)
                        norm(cy, cy, mv3, rs3).then_inc(p_xc, 1)
                        need(pool, p_xc, gC, 2, l + 1)
                        pool.tensor_tensor(cy, cy, over_graphs(cg_row[:, l, :]), ALU.mult).then_inc(p_cg, 1)
                        need(pool, p_cg, gC, 2, l + 1)
                        pool.tensor_tensor(x2 if l == 0 else cy, cy, over_graphs(cb_row[:, l, :]),
                                           ALU.add).then_inc(p_c, 1)
                    if step == "A.wo" and gA is not None:
                        need(pool, d_mv2, gA, B, B)
                        rsqrt(gA, 1, 1, mv2, ve2, rs2, p_ve2, p_rs2)
                        need(pool, t_xT, g0, 1, 1)
                        norm(xhat, x1, mv2, rs2).then_inc(p_x2, 1)
                        need(pool, d_x2, gM, 1, 1)
                        pool.tensor_tensor(x1b, x1, over_graphs(b2_row[:, :]), ALU.add).then_inc(p_x1b, 1)

            run(pool, iteration)

        @block.scalar
        def _(act):
            act.wait_ge(prep_dve, PREP_DVE)
            act.wait_ge(const_ok, 6)

            def iteration(it, odd):
                g0, gA, gM, gC = groups(it, odd)

                def exps(b):
                    need(act, d_nb, gA, B, b + 1)
                    for h in range(H):
                        last = act.activation(sc[:, b % 2, h], sc[:, b % 2, h], ACT.Exp,
                                              bias=nbias[:, b, h:h + 1])
                    last.then_inc(a_exp, 1)

                for step in ORDER:
                    stage, what = step.split(".")
                    if stage == "A0" and g0 is not None:
                        need(act, t_xT, g0, 1, 1)
                        need(act, t_v, g0, 2, 0)
                        act.copy(xT_h[:, :, :], psC).then_inc(a_xT, 1)
                    if stage == "A" and gA is not None:
                        if what in ("q0", "q1", "k0", "k1"):
                            i = ("q0", "q1", "k0", "k1").index(what)
                            need(act, t_qk, gA, 4, i + 1)
                            need(act, t_AV, gA, 4, 0)
                            src = (psA1, psA[:, 0, :], psA[:, 1, :], psA1)[i]
                            act.activation(qk16[:, 0, i, :], src, ACT.Identity,
                                           bias=bqk_col[:, i:i + 1]).then_inc(a_qk, 1)
                        elif what in ("v0", "v1"):
                            n = int(what[1])
                            need(act, t_v, gA, 2, n + 1)
                            act.copy(v_h[:, 2 * n:2 * n + 2, :, 0:HD].rearrange("p b h d -> p (b h) d"),
                                     psA[:, n, :].rearrange("p (n d) -> p n d", d=HD)).then_inc(a_v, 1)
                        elif what[:2] == "PT":
                            b = int(what[2])
                            need(act, t_PT, gA, B, b + 1)
                            need(act, t_AV, gA, B, b - 1)
                            act.copy(pT16[:, b % 2, 0], psA_heads).then_inc(a_PT, 1)
                        elif what == "oT":
                            need(act, t_oT, gA, 1, 1)
                            need(act, t_up, gM, FC, FC)
                            act.copy(rot_h[:, :, :], psA).then_inc(a_oT, 1)
                    if stage == "M" and gM is not None:
                        if what == "xT":
                            need(act, t_mT, gM, 1, 1)
                            act.copy(rot_h[:, :, :], psM).then_inc(a_mT, 1)
                        elif what[:2] == "up":
                            c = int(what[2])
                            need(act, t_up, gM, FC, c + 1)
                            need(act, d_lo, gM, FC, c - 1)
                            act.activation(hidden[:, c % 2, :], psUp[c % 2], ACT.Gelu,
                                           bias=b1_col[:, c:c + 1]).then_inc(a_gelu, 1)
                    if stage in ("C0", "C1") and gC is not None:
                        l = int(stage[1])
                        if what == "xT":
                            need(act, t_cT, gC, 2, l + 1)
                            need(act, t_cW, gC, 2, l)
                            act.copy(cT_h[:, :, :], psC).then_inc(a_cT, 1)
                        elif what in "qk":
                            i = "qk".index(what)
                            need(act, t_cqk, gC, 4, 2 * l + i + 1)
                            need(act, t_cS, gC, 2, l)
                            act.activation((cq, ck)[i][:, :], psC[:, i, :], ACT.Identity,
                                           bias=cb_col[:, i, l:l + 1]).then_inc(a_cqk, 1)
                        elif what == "S":
                            need(act, d_cnb, gC, 2, l + 1)
                            for b in range(B):
                                last = act.activation(cs[:, b], cs[:, b], ACT.Exp, bias=cmax[:, b:b + 1],
                                                      accum_out=csum[:, b:b + 1])
                            last.then_inc(a_cexp, 1)
                        elif what == "xW":
                            need(act, t_cW, gC, 2, l + 1)
                            need(act, t_cPV, gC, 2, l)
                            act.copy(cW, psC_rows).then_inc(a_cW, 1)
                        elif what == "PT":
                            need(act, t_cPT, gC, 2, l + 1)
                            act.copy(cPT, psC_PT).then_inc(a_cPT, 1)
                    if gA is not None and step in ("C1.xT", "C1.k", "M.down5", "A.S3"):
                        exps(("C1.xT", "C1.k", "M.down5", "A.S3").index(step))

            run(act, iteration)

        @block.vector
        def _(dve):
            made = [0]

            def prep(instruction):
                made[0] += 1
                instruction.then_inc(prep_dve, 1)

            def split(hi, lo, raw, gain=None, scale=1.0):
                if gain is None:
                    prep(dve.tensor_scalar(hi, raw, scale, None, ALU.mult))
                    dve.wait_ge(prep_dve, made[0])
                    prep(dve.scalar_tensor_tensor(lo, raw, scale, hi.bitcast(F32), ALU.mult, ALU.subtract))
                else:
                    assert scale == 1.0
                    prep(dve.tensor_scalar(hi, raw, gain, None, ALU.mult))
                    dve.wait_ge(prep_dve, made[0])
                    prep(dve.scalar_tensor_tensor(lo, raw, gain, hi.bitcast(F32), ALU.mult, ALU.subtract))

            QSCALE, CSCALE = 1 / math.sqrt(HD), 1 / math.sqrt(P)

            def stats(g, per, k0, rows, st, mv, st_ok, mv_ok):
                for b in range(B):
                    dve.bn_stats(st[:, b, :], rows[:, b, :]).then_inc(st_ok, 1)
                need(dve, st_ok, g, per, k0 + B)
                apart(dve)
                for b in range(B):
                    dve.bn_aggr(mv[:, b, :], st[:, b, :]).then_inc(mv_ok, 1)

            dve.wait_ge(ld_vec, 16 * NVEC)
            prep(dve.tensor_scalar(ln_q[:, :], ln_col[:, 0, :], QSCALE, None, ALU.mult))
            dve.wait_ge(prep_dve, made[0])
            dve.wait_ge(prep_pe, 1)
            prep(dve.tensor_tensor(bqk_col[:, :], bqk_col[:, :], ps[:, 0, 0:4], ALU.add))
            prep(dve.tensor_tensor(bv_col[:, :], bv_col[:, :], ps[:, 0, 4:6], ALU.add))
            dve.wait_ge(prep_dve, made[0])
            prep(dve.tensor_scalar(bqk_col[:, 0:2], bqk_col[:, 0:2], QSCALE, None, ALU.mult))
            prep(dve.tensor_copy(bv_rep[:, :, :], bv_col[:, :].unsqueeze(2).broadcast_to([P, KC, P])))
            for c in range(KC):
                split(wqk_h[:, c, 0:D], wqk_l[:, c, 0:D], raw_qkvo[:, 0, c], ln_q[:, c:c + 1])
                split(wqk_h[:, c, D:2 * D], wqk_l[:, c, D:2 * D], raw_qkvo[:, 1, c], ln_col[:, 0, c:c + 1])
                split(wv_h[:, c], wv_l[:, c], raw_qkvo[:, 2, c], ln_col[:, 0, c:c + 1])
            dve.wait_ge(prep_pe, 2)
            prep(dve.tensor_tensor(bo_row[:, :], bo_row[:, :], ps[:, 1, 0:D], ALU.add))
            split(wo_h[:, :, :], wo_l[:, :, :], raw_qkvo[:, 3])
            dve.wait_ge(prep_pe, 3)
            prep(dve.tensor_tensor(b1_col[:, :], b1_col[:, :], ps[:, 2, 0:FC], ALU.add))
            for c in range(KC):
                split(w1_h[:, c], w1_l[:, c], raw_w1[:, c], ln_col[:, 2, c:c + 1])
            prep(dve.tensor_scalar(cb_col[:, 0, :], cb_col[:, 0, :], CSCALE, None, ALU.mult))
            dve.wait_ge(prep_pe, 4)
            for l in range(L):
                qk = ps[:, 3 + l, :].rearrange("p (w c f) -> p w c f", w=2, c=KC)
                split(cqk_h[:, l, :, 0:P], cqk_l[:, l, :, 0:P], qk[:, 0], scale=CSCALE)
                split(cqk_h[:, l, :, P:2 * P], cqk_l[:, l, :, P:2 * P], qk[:, 1])
                split(cw_h[:, l], cw_l[:, l], ps[:, 5 + l, :].rearrange("p (c e) -> p c e", c=KC))
            dve.wait_ge(ld_raw[2], 16)
            split(w2_h[:, :, :], w2_l[:, :, :], raw_w2)
            assert made[0] == PREP_DVE, made[0]
            dve.wait_ge(const_ok, 6)

            def iteration(it, odd):
                g0, gA, gM, gC = groups(it, odd)
                for step in ORDER:
                    stage, what = step.split(".")
                    if step == "A.q0" and gA is not None:
                        need(dve, ld_adjA, gA, 16, 16)
                        need(dve, d_S, gA, B, 0)
                        dve.tensor_scalar(mtmp[:, :, :], adjA[:, :, :], 0, -1.0, ALU.is_gt, ALU.add)\
                           .then_inc(d_mt, 1)
                        dve.scalar_tensor_tensor(biasA[:, :, :], adjA[:, :, :], 0.1, adjA[:, :, :],
                                                 ALU.mult, ALU.mult).then_inc(d_mt, 1)
                        need(dve, d_mt, gA, 2, 2)
                        dve.scalar_tensor_tensor(biasA[:, :, :], mtmp[:, :, :], -MASKED, biasA[:, :, :],
                                                 ALU.mult, ALU.add).then_inc(d_mA, 1)
                        need(dve, d_mA, gA, 1, 1)
                    if step == "A.q0" and gC is not None:
                        need(dve, ld_adjC, gC, 16, 16)
                        need(dve, d_cS, gC, 2, 0)
                        dve.tensor_scalar(biasC[:, :, :], adjC[:, :, :], 0, MASKED, ALU.is_equal, ALU.mult)\
                           .then_inc(d_mC, 1)
                        need(dve, d_mC, gC, 1, 1)
                    if step == "A.v0" and g0 is not None:
                        need(dve, ld_x[g0[1]], (g0[0], 0), 8, 16)
                        need(dve, p_x1, g0, 1, 0)
                        stats(g0, B, 0, xin[:, g0[1]], st1, mv1, d_st1, d_mv1)
                    if stage == "A0" and g0 is not None:
                        need(dve, a_xT, g0, 1, 1)
                        dve.tensor_tensor(xT_l[:, :, :], psC, xT_h[:, :, :].bitcast(F32), ALU.subtract)\
                           .then_inc(d_xT, 1)
                    if stage == "A" and gA is not None:
                        if what in ("q0", "q1", "k0", "k1"):
                            i = ("q0", "q1", "k0", "k1").index(what)
                            need(dve, a_qk, gA, 4, i + 1)
                            src = (psA1, psA[:, 0, :], psA[:, 1, :], psA1)[i]
                            dve.scalar_tensor_tensor(qk16[:, 1, i, :], src, bqk_col[:, i:i + 1],
                                                     qk16[:, 0, i, :], ALU.add, ALU.subtract).then_inc(d_qk, 1)
                        elif what in ("v0", "v1"):
                            n = int(what[1])
                            need(dve, a_v, gA, 2, n + 1)
                            dve.tensor_tensor(
                                v_l[:, 2 * n:2 * n + 2, :, 0:HD].rearrange("p b h d -> p (b h) d"),
                                psA[:, n, :].rearrange("p (n d) -> p n d", d=HD),
                                v_h[:, 2 * n:2 * n + 2, :, 0:HD].rearrange("p b h d -> p (b h) d"),
                                ALU.subtract).then_inc(d_v, 1)
                        elif what[0] == "S":
                            b = int(what[1])
                            need(dve, t_S, gA, B, b + 1)
                            need(dve, t_PT, gA, B, b - 1)
                            if b == 0:
                                need(dve, d_lo, gM, FC, FC)
                            dve.tensor_tensor(sc[:, b % 2], psA_heads,
                                              biasA[:, b].unsqueeze(1).broadcast_to([P, H, P]),
                                              ALU.add).then_inc(d_S, 1)
                            need(dve, d_S, gA, B, b + 1)
                            dve.tensor_reduce(nmax[:, b, :], sc[:, b % 2], AX.X, ALU.max).then_inc(d_max, 1)
                            need(dve, d_max, gA, B, b + 1)
                            dve.tensor_scalar(nbias[:, b, :], nmax[:, b, :], -1.0, P_SCALE,
                                              ALU.mult, ALU.add).then_inc(d_nb, 1)
                        elif what[:2] == "PT":
                            b = int(what[2])
                            need(dve, a_PT, gA, B, b + 1)
                            dve.tensor_tensor(pT16[:, b % 2, 1], psA_heads, pT16[:, b % 2, 0], ALU.subtract)\
                               .then_inc(d_PT, 1)
                        elif what[:2] == "AV":
                            b = int(what[2])
                            need(dve, t_AV, gA, B, b + 1)
                            dve.reciprocal(rec[:, b, :], psAV[:, :, HD]).then_inc(d_rec, 1)
                            need(dve, d_rec, gA, B, b + 1)
                            if b == 0:
                                need(dve, p_x1b, gA, 1, 0)
                            dve.tensor_tensor(o_rows[:, b].rearrange("p (h d) -> p h d", h=H),
                                              psAV[:, :, 0:HD],
                                              rec[:, b, :].unsqueeze(2).broadcast_to([P, H, HD]),
                                              ALU.mult).then_inc(d_o, 1)
                        elif what == "oT":
                            need(dve, a_oT, gA, 1, 1)
                            dve.tensor_tensor(rot_l[:, :, :], psA, rot_h[:, :, :].bitcast(F32), ALU.subtract)\
                               .then_inc(d_oT, 1)
                        elif what == "wo":
                            need(dve, t_wo, gA, 1, 1)
                            need(dve, p_xb, gA, 1, 1)
                            dve.tensor_tensor(x1, psA_rows, xin[:, gA[1]], ALU.add).then_inc(d_x1, 1)
                            need(dve, d_x1, gA, 1, 1)
                            need(dve, p_x2, gA, 1, 0)
                            stats(gA, B, 0, x1, st2, mv2, d_st2, d_mv2)
                    if stage == "M" and gM is not None:
                        if what == "xT":
                            need(dve, a_mT, gM, 1, 1)
                            dve.tensor_tensor(rot_l[:, :, :], psM, rot_h[:, :, :].bitcast(F32), ALU.subtract)\
                               .then_inc(d_mT, 1)
                        elif what[:2] == "up":
                            c = int(what[2])
                            need(dve, a_gelu, gM, FC, c + 1)
                            need(dve, t_down, gM, FC, c + 1 - RING)
                            dve.tensor_copy(hid_h[:, c % RING, :], hidden[:, c % 2, :]).then_inc(d_hi, 1)
                            need(dve, d_hi, gM, FC, c + 1)
                            dve.tensor_tensor(hid_l[:, c % RING, :], hidden[:, c % 2, :],
                                              hid_h[:, c % RING, :].bitcast(F32), ALU.subtract)\
                               .then_inc(d_lo, 1)
                        elif what == "down7":
                            need(dve, t_down, gM, FC, FC)
                            need(dve, p_x1b, gM, 1, 1)
                            need(dve, d_cy, gC, 2 * B, 2 * B)
                            dve.tensor_tensor(x2, psM_rows, x1b, ALU.add).then_inc(d_x2, 1)
                    if stage in ("C0", "C1") and gC is not None:
                        l = int(stage[1])
                        if what == "xT":
                            need(dve, a_cT, gC, 2, l + 1)
                            dve.tensor_tensor(cT_l[:, :, :], psC, cT_h[:, :, :].bitcast(F32), ALU.subtract)\
                               .then_inc(d_cT, 1)
                        elif what == "S":
                            need(dve, t_cS, gC, 2, l + 1)
                            need(dve, t_cPT, gC, 2, l)
                            dve.tensor_tensor(cs, psC_S, biasC[:, :, :], ALU.add).then_inc(d_cS, 1)
                            need(dve, d_cS, gC, 2, l + 1)
                            dve.tensor_reduce(crec[:, :], cs, AX.X, ALU.max).then_inc(d_cmax, 1)
                            need(dve, d_cmax, gC, 2, l + 1)
                            dve.tensor_scalar(cmax[:, :], crec[:, :], -1.0, None, ALU.mult).then_inc(d_cnb, 1)
                        elif what == "PV":
                            need(dve, a_cexp, gC, 2, l + 1)
                            dve.reciprocal(crec[:, :], csum[:, :]).then_inc(d_crec, 1)
                            need(dve, d_crec, gC, 2, l + 1)
                            dve.scalar_tensor_tensor(cscale[:, :], cmax[:, :], -MASKED / 10, crec[:, :],
                                                     ALU.is_lt, ALU.mult).then_inc(d_csc, 1)
                            need(dve, d_csc, gC, 2, l + 1)
                            need(dve, t_cPV, gC, 2, l + 1)
                            if l == 0:
                                need(dve, st_out, gC, 16, 0)
                            for b in range(B):
                                dve.scalar_tensor_tensor(cy[:, b], psC_rows[:, b], cscale[:, b:b + 1],
                                                         x2[:, b], ALU.mult, ALU.add).then_inc(d_cy, 1)
                            need(dve, d_cy, gC, 2 * B, B * l + B)
                            stats(gC, 2 * B, B * l, cy, st3, mv3, d_cst, d_cmv)

            run(dve, iteration)

        @block.tensor
        def _(pe):
            pe.wait_ge(const_ok, 6)
            pe.wait_ge(ld_vec, 16 * NVEC)
            pe.wait_ge(ld_raw[0], 16 * 4)
            for t in range(6):
                for c in range(KC):
                    last = pe.matmul(ps[:, 0, t:t + 1], raw_qkvo[:, t // 2, c, (t % 2) * P:(t % 2) * P + P],
                                     ln_col[:, 1, c:c + 1], start=(c == 0), stop=(c == KC - 1))
            last.then_inc(prep_pe, 1)
            pe.wait_ge(prep_dve, 5)
            for c in range(KC):
                last = pe.matmul(ps[:, 1, 0:D], bv_rep[:, c], raw_qkvo[:, 3, c],
                                 start=(c == 0), stop=(c == KC - 1))
            last.then_inc(prep_pe, 1)
            pe.wait_ge(ld_raw[1], 16)
            for t in range(FC):
                for c in range(KC):
                    last = pe.matmul(ps[:, 2, t:t + 1], raw_w1[:, c, t * P:t * P + P],
                                     ln_col[:, 3, c:c + 1], start=(c == 0), stop=(c == KC - 1))
            last.then_inc(prep_pe, 1)
            pe.wait_ge(ld_raw[3], 16 * 3 * L)
            for l in range(L):
                for w in range(2):
                    for c in range(KC):
                        pe.transpose(ps[:, 3 + l, (w * KC + c) * P:(w * KC + c + 1) * P],
                                     raw_cqk[:, l, w, c * P:(c + 1) * P], ident[:, :])
                for c in range(KC):
                    for e in range(KC):
                        last = pe.transpose(ps[:, 5 + l, c * D + e * P:c * D + (e + 1) * P],
                                            raw_cw[:, l, e, c * P:(c + 1) * P], ident[:, :])
            last.then_inc(prep_pe, 1)
            pe.wait_ge(prep_dve, PREP_DVE)

            def transposes(dst, rows, signal):
                for c in range(KC):
                    for b in range(B):
                        last = pe.transpose(dst[:, c, b * P:(b + 1) * P], rows[:, b, c * P:(c + 1) * P],
                                            ident[:, :])
                last.then_inc(signal, 1)

            def to_columns(dst, w_h, w_l, x_h, x_l, n):
                for c in range(KC):
                    last = mm3(pe, dst, w_h[:, c, n:n + P], w_l[:, c, n:n + P], x_h[:, c, :], x_l[:, c, :],
                               start=(c == 0), stop=(c == KC - 1))
                return last

            def to_rows(dst, x_h, x_l, w_h, w_l, b):
                for c in range(KC):
                    last = mm3(pe, dst, x_h[:, c, b * P:(b + 1) * P], x_l[:, c, b * P:(b + 1) * P],
                               w_h[:, c, :], w_l[:, c, :], start=(c == 0), stop=(c == KC - 1))
                return last

            def iteration(it, odd):
                g0, gA, gM, gC = groups(it, odd)
                for step in ORDER:
                    stage, what = step.split(".")
                    if stage == "A0" and g0 is not None:
                        need(pe, p_x1, g0, 1, 1)
                        need(pe, d_cy, gC, 2 * B, 2 * B)
                        need(pe, d_xT, g0, 1, 0)
                        transposes(psC, xhat, t_xT)
                    if stage == "A" and gA is not None:
                        if what in ("q0", "q1", "k0", "k1"):
                            i = ("q0", "q1", "k0", "k1").index(what)
                            if i == 0:
                                need(pe, a_xT, gA, 1, 1)
                                need(pe, d_xT, gA, 1, 1)
                                need(pe, d_o, gA, B, 0)
                            if i == 1:
                                need(pe, d_x1, gA, 1, 0)
                            if i == 3:
                                need(pe, d_qk, gA, 4, 1)
                            dst = (psA1, psA[:, 0, :], psA[:, 1, :], psA1)[i]
                            to_columns(dst, wqk_h, wqk_l, xT_h, xT_l, i * P).then_inc(t_qk, 1)
                        elif what in ("v0", "v1"):
                            n = int(what[1])
                            need(pe, d_qk, gA, 4, 2 + n)
                            for b in (2 * n, 2 * n + 1):
                                last = to_rows(psA_rows[:, b], xT_h, xT_l, wv_h, wv_l, b)
                            last.then_inc(t_v, 1)
                        elif what[0] == "S":
                            b = int(what[1])
                            if b == 0:
                                need(pe, stk, gA, STK, STK)
                                need(pe, d_v, gA, 2, 2)
                            else:
                                need(pe, d_S, gA, B, b)
                                if b >= 2:
                                    need(pe, d_PT, gA, B, b - 1)
                            for h in range(H):
                                last = pe.matmul(psA_heads[:, h], qS[0:96, h // 4, h % 4, b * P:(b + 1) * P],
                                                 kS[0:96, h // 4, h % 4, b * P:(b + 1) * P],
                                                 start=True, stop=True)
                            last.then_inc(t_S, 1)
                        elif what[:2] == "PT":
                            b = int(what[2])
                            need(pe, a_exp, gA, B, b + 1)
                            need(pe, d_S, gA, B, min(b + 2, B))
                            if b > 0:
                                need(pe, d_PT, gA, B, b)
                            for h in range(H):
                                last = pe.transpose(psA_heads[:, h], sc[:, b % 2, h], ident[:, :])
                            last.then_inc(t_PT, 1)
                        elif what[:2] == "AV":
                            b = int(what[2])
                            need(pe, d_PT, gA, B, b + 1)
                            if b == 0:
                                need(pe, a_gelu, gM, FC, FC)
                            need(pe, d_o, gA, B, b)
                            for h in range(H):
                                last = mm3(pe, psAV[:, h, 0:HD + 1], pT16[:, b % 2, 0, h], pT16[:, b % 2, 1, h],
                                           v_h[:, b, h, 0:HD + 1], v_l[:, b, h, 0:HD + 1],
                                           start=True, stop=True)
                            last.then_inc(t_AV, 1)
                        elif what == "oT":
                            need(pe, d_o, gA, B, B)
                            need(pe, d_PT, gA, B, B)
                            transposes(psA, o_rows, t_oT)
                        elif what == "wo":
                            need(pe, d_oT, gA, 1, 1)
                            for b in range(B):
                                last = to_rows(psA_rows[:, b], rot_h, rot_l, wo_h, wo_l, b)
                            last.then_inc(t_wo, 1)
                    if stage == "M" and gM is not None:
                        if what == "xT":
                            need(pe, p_x2, gM, 1, 1)
                            need(pe, d_x2, gM, 1, 0)
                            transposes(psM, xhat, t_mT)
                        elif what[:2] == "up":
                            c = int(what[2])
                            if c == 0:
                                need(pe, d_mT, gM, 1, 1)
                            if c == 1:
                                need(pe, d_qk, gA, 4, 4)
                                need(pe, d_o, gM, B, B)
                            need(pe, a_gelu, gM, FC, c - 1)
                            to_columns(psUp[c % 2], w1_h, w1_l, rot_h, rot_l, c * P).then_inc(t_up, 1)
                        elif what[:4] == "down":
                            c = int(what[4])
                            need(pe, d_lo, gM, FC, c + 1)
                            for b in range(B):
                                last = mm3(pe, psM_rows[:, b], hid_h[:, c % RING, b * P:(b + 1) * P],
                                           hid_l[:, c % RING, b * P:(b + 1) * P], w2_h[:, c, :], w2_l[:, c, :],
                                           start=(c == 0 and b % 2 == 0), stop=(c == FC - 1),
                                           skip_group_check=True)
                            last.then_inc(t_down, 1)
                    if stage in ("C0", "C1") and gC is not None:
                        l = int(stage[1])
                        if what == "xT":
                            if l == 0:
                                need(pe, d_x2, gC, 1, 1)
                                need(pe, d_xT, gA, 1, 1)
                                need(pe, d_cy, gC, 2 * B, 0)
                            else:
                                need(pe, p_c, gC, 2, 1)
                                need(pe, d_cy, gC, 2 * B, B)
                            transposes(psC, x2, t_cT)
                        elif what in "qk":
                            i = "qk".index(what)
                            need(pe, d_cT, gC, 2, l + 1)
                            to_columns(psC[:, i, :], cqk_h[:, l], cqk_l[:, l], cT_h, cT_l, i * P)\
                                .then_inc(t_cqk, 1)
                        elif what == "S":
                            need(pe, a_cqk, gC, 4, 2 * l + 2)
                            for b in range(B):
                                last = pe.matmul(psC_S[:, b], cq[:, b * P:(b + 1) * P], ck[:, b * P:(b + 1) * P],
                                                 start=True, stop=True)
                            last.then_inc(t_cS, 1)
                        elif what == "xW":
                            need(pe, d_cS, gC, 2, l + 1)
                            for b in range(B):
                                last = to_rows(psC_rows[:, b], cT_h, cT_l, cw_h[:, l], cw_l[:, l], b)
                            last.then_inc(t_cW, 1)
                        elif what == "PT":
                            need(pe, a_cexp, gC, 2, l + 1)
                            need(pe, a_cW, gC, 2, l + 1)
                            for b in range(B):
                                last = pe.transpose(psC_PT[:, b], cs[:, b], ident[:, :])
                            last.then_inc(t_cPT, 1)
                        elif what == "PV":
                            need(pe, a_cPT, gC, 2, l + 1)
                            for b in range(B):
                                last = pe.matmul(psC_rows[:, b], cPT[:, b], cW[:, b], start=True, stop=True)
                            last.then_inc(t_cPV, 1)

            run(pe, iteration)


_INS = ["x", "adj", "L0_gnn_ln1_g", "L0_gnn_ln1_b", "L0_gnn_ln2_g", "L0_gnn_ln2_b", "L0_gnn_wq",
        "L0_gnn_bq", "L0_gnn_wk", "L0_gnn_bk", "L0_gnn_wv", "L0_gnn_bv", "L0_gnn_wo", "L0_gnn_bo",
        "L0_gnn_w1", "L0_gnn_b1", "L0_gnn_w2", "L0_gnn_b2", "L1_gnn_Wq", "L1_gnn_bq", "L1_gnn_bk",
        "L1_gnn_Wk", "L1_gnn_Wc", "L1_gnn_ln_g", "L1_gnn_ln_b"]


def kernel(**inputs):
    import numpy as _np
    import concourse.bacc as _bacc
    from concourse.bass_utils import run_bass_kernel_spmd as _run

    nc = _bacc.Bacc("TRN2", target_bir_lowering=False, num_devices=1)
    arrays, args = {}, []
    for name in _INS:
        a = _np.ascontiguousarray(inputs[name])
        arrays[f"in_{name}"] = a
        args.append(nc.dram_tensor(f"in_{name}", a.shape, mybir.dt.from_np(a.dtype), kind="ExternalInput").ap())
    args.append(nc.dram_tensor("out_0", inputs["x"].shape, F32, kind="ExternalOutput").ap())
    graph_blocks(nc, *args)
    r = _run(nc, [arrays], core_ids=[0])
    return r.results[0]["out_0"]
```

```python
import math
from contextlib import ExitStack

import concourse.bass as bass
from concourse import mybir

F32, F32R, F16, BF16, I32 = (mybir.dt.float32, mybir.dt.float32r, mybir.dt.float16,
                             mybir.dt.bfloat16, mybir.dt.int32)
ALU, ACT, AX = mybir.AluOpType, mybir.ActivationFunctionType, mybir.AxisListType

P = 128
D = 256
KC = D // P
H, HD = 8, 32
FF = 4 * D
FC = FF // P
B = 4
R = B * P
L = 2
VW = HD + 2
EPS = 1e-5
MASKED = -1e30
P_SCALE = math.log(1024.0)
RING = 3

TENSOR = ["Q.k0+0", "M.down2-2", "A.S2-1", "M.up4-2", "C0.q-3", "A.PT1-1", "M.down3-2", "M.up5-2",
          "C0.k-3", "Q.q0+0", "M.up6-2", "C0.S-3", "M.down4-2", "A.S3-1", "C0.xW-3", "Q.q1+0",
          "A.AV0-1", "A.PT2-1", "M.down5-2", "A.AV1-1", "Q.k1+0", "C0.PT-3", "A.PT3-1", "A.AV2-1",
          "C1.xT-4", "M.up7-2", "A.AV3-1", "M.down6-2", "A.oT-1", "C0.PV-3", "M.down7-2", "A.wo-1",
          "C1.q-4", "C1.k-4", "A.S0+0", "C1.S-4", "Q.v1+0", "C1.xW-4", "M.mT-1", "A.S1+0",
          "C1.PT-4", "Q.v0+0", "M.up0-1", "C1.PV-4", "A.PT0+0", "M.up1-1", "N.xT+1", "M.down0-1",
          "M.up2-1", "M.down1-1", "C0.xT-2", "M.up3-1"]
SCALAR = ["C0.xT-3", "M.up3-2", "A.exp1-1", "M.up4-2", "C0.q-3", "Q.k0+0", "M.up5-2", "C0.k-3",
          "A.PT1-1", "Q.q0+0", "M.up6-2", "A.exp2-1", "C0.ex-3", "Q.q1+0", "C0.xW-3", "A.PT2-1",
          "A.exp3-1", "Q.k1+0", "C0.PT-3", "A.PT3-1", "C1.xT-4", "M.up7-2", "A.oT-1", "C1.q-4",
          "C1.k-4", "Q.v1+0", "C1.ex-4", "C1.xW-4", "M.mT-1", "C1.PT-4", "A.exp0+0", "M.up0-1",
          "Q.v0+0", "M.up1-1", "A.PT0+0", "N.xT+1", "M.up2-1"]
VECTOR = ["A.PT1-1", "C0.S-3", "C0.max-3", "Q.q0+0", "A.S3-1", "A.max3-1", "A.AV0-1", "M.lo6-2",
          "Q.q1+0", "A.PT2-1", "A.AV1-1", "Q.k1+0", "A.AV2-1", "A.PT3-1", "C1.xT-4", "A.AV3-1",
          "Q.mA+0", "A.oT-1", "C0.PV-3", "M.x2-2", "A.wo-1", "A.st-1", "A.S0+0", "C1.S-4",
          "C1.max-4", "A.xh-1", "A.max0+0", "N.st+1", "Q.v1+0", "M.mT-1", "A.S1+0", "N.xh+1",
          "C1.PV-4", "M.lo0-1", "A.max1+0", "Q.v0+0", "M.mC-2", "N.xT+1", "A.PT0+0", "M.lo2-1",
          "C1.st-4", "C0.xT-2", "A.S2+0", "C0.st-3", "C1.xh-4", "M.lo4-1", "Q.k0+1", "C0.xh-3",
          "A.max2+0"]
GPSIMD = ["M.lo1-1", "M.lo3-1", "N.xb+1", "C1.rs-4", "C0.rs-3", "C1.af-4", "M.lo5-1", "A.x1b-1",
          "C0.af-3", "M.lo7-1", "A.rs+0", "C1.cWb-3", "N.rs+2"]
SYNC = ["Q.ldA+0", "Q.stk+0", "N.ld+1", "M.ldC-2", "C1.sto-4"]

QK = ("q0", "q1", "k0", "k1")


def graph_blocks(nc, x, adj, ln1_g, ln1_b, ln2_g, ln2_b, wq, bq, wk, bk, wv, bv, wo, bo, w1, b1,
                 w2, b2, cWq, cbq, cbk, cWk, cWc, c_g, c_b, out):
    NG = x.shape[0] // B
    x_dram = x.rearrange("(g t b) p d -> g t p b d", t=2, b=B)
    adj_dram = adj.rearrange("(g t b) p k -> g t p b k", t=2, b=B)
    out_dram = out.rearrange("(g t b) p d -> g t p b d", t=2, b=B)

    with ExitStack() as ctx:
        def sb(name, shape, dt=F32):
            return ctx.enter_context(nc.sbuf_tensor(name, shape, dt))

        def sem(name):
            return ctx.enter_context(nc.semaphore(name))

        ident = sb("ident", [P, P])
        wqk_h, wqk_l = sb("wqk_h", [P, KC, 2 * D], F32R), sb("wqk_l", [P, KC, 2 * D], F32R)
        wv_h, wv_l = sb("wv_h", [P, KC, D], F32R), sb("wv_l", [P, KC, D], F32R)
        wo_h, wo_l = sb("wo_h", [P, KC, D], F32R), sb("wo_l", [P, KC, D], F32R)
        w1_h, w1_l = sb("w1_h", [P, KC, FF], F32R), sb("w1_l", [P, KC, FF], F32R)
        w2_h, w2_l = sb("w2_h", [P, FC, D], F32R), sb("w2_l", [P, FC, D], F32R)
        cqk_h, cqk_l = sb("cqk_h", [P, L, KC, 2 * P], F32R), sb("cqk_l", [P, L, KC, 2 * P], F32R)
        cw_h, cw_l = sb("cw_h", [P, L, KC, D], F32R), sb("cw_l", [P, L, KC, D], F32R)
        ln_col = sb("ln_col", [P, 4, KC])
        bqk_col = sb("bqk_col", [P, 4])
        bv_col = sb("bv_col", [P, KC])
        b1_col = sb("b1_col", [P, FC])
        cb_col = sb("cb_col", [P, 2, L])
        ln_q = sb("ln_q", [P, KC])
        cln_col = sb("cln_col", [P, 2, KC])
        cgq = sb("cgq", [P, KC])
        bo_row, b2_row = sb("bo_row", [P, D]), sb("b2_row", [P, D])
        cg_row, cb_row = sb("cg_row", [P, L, D]), sb("cb_row", [P, L, D])
        cwb_row = sb("cwb_row", [P, D])
        minus_half, eps_cols = sb("minus_half", [P, B]), sb("eps_cols", [P, B])

        area = sb("area", [P, 8192])
        sc = area[:, 0:2048].rearrange("p (s h k) -> p s h k", s=2, h=H)
        xhat = area[:, 2048:3072].rearrange("p (b d) -> p b d", b=B)
        o_rows = xhat
        x1 = area[:, 3072:4096].rearrange("p (b d) -> p b d", b=B)
        x2 = area[:, 4096:5120].rearrange("p (b d) -> p b d", b=B)
        xhatN = area[:, 5120:6144].rearrange("p (b d) -> p b d", b=B)
        cW = area[:, 6144:7168].rearrange("p (b d) -> p b d", b=B)
        hidden = area[:, 7168:8192].rearrange("p (s n) -> p s n", s=2)
        raw_qkvo = area[:, 0:2048].rearrange("p (w c n) -> p w c n", w=4, c=KC)
        raw_w1 = area[:, 2048:4096].rearrange("p (c n) -> p c n", c=KC)
        raw_w2 = area[:, 4096:6144].rearrange("p (c n) -> p c n", c=FC)
        raw_cqk = area[:, 6144:7168].rearrange("p (l w n) -> p l w n", l=L, w=2)
        raw_cw = area[:, 7168:8192].rearrange("p (l c n) -> p l c n", l=L, c=KC)

        xin = sb("xin", [P, 2, B, D])
        xT_h, xT_l = sb("xT_h", [P, KC, R], F32R), sb("xT_l", [P, KC, R], F32R)
        qk16 = sb("qk16", [P, 4, 2, R], F16)
        pT16 = sb("pT16", [P, 2, 2, H, P], F16)
        qkS = sb("qkS", [P, 2, 4, 2, R], F16)
        v_h, v_l = sb("v_h", [P, B, H, VW], F16), sb("v_l", [P, B, H, VW], F16)
        rot_h, rot_l = sb("rot_h", [P, KC, R], F32R), sb("rot_l", [P, KC, R], F32R)
        hid_h, hid_l = sb("hid_h", [P, RING, R], F32R), sb("hid_l", [P, RING, R], F32R)
        cT_h, cT_l = sb("cT_h", [P, KC, R], F32R), sb("cT_l", [P, KC, R], F32R)
        cq, ck = sb("cq", [P, R]), sb("ck", [P, R])
        cs = sb("cs", [P, L, B, P])
        xh3, x3 = sb("xh3", [P, B, D]), sb("x3", [P, B, D])
        bv_rep = xh3[:, 0, :].rearrange("p (c n) -> p c n", c=KC)
        cb_rep = xh3[:, 1, :].rearrange("p (c n) -> p c n", c=KC)
        cqkT = x3[:, 0:2, :].rearrange("p w (c f) -> p w c f", c=KC)
        cwT = x3[:, 2:4, :]
        adj_in = sb("adj_in", [P, B, P], I32)
        biasA, biasC = sb("biasA", [P, B, P]), sb("biasC", [P, 2, B, P], BF16)
        nmax = sb("nmax", [P, B, H])
        nbias = sb("nbias", [P, B, H])
        rec = sb("rec", [P, B, H])
        st, mv = sb("st", [P, 4, B, 6]), sb("mv", [P, 4, B, 2])
        ve, rs = sb("ve", [P, 4, B]), sb("rs", [P, 4, B])
        cmax, csum, crec, cscale = (sb(n, [P, L, B]) for n in ("cmax", "csum", "crec", "cscale"))
        cneg = sb("cneg", [P, L, B])

        ps = ctx.enter_context(nc.psum_tensor("ps", [P, 8, 512], F32))
        psA = ps[:, 0:2, :]
        psUp = ps[:, 3, :]
        psQ = (ps[:, 2, :], ps[:, 3, :])
        psM = ps[:, 4:6, :]
        psC = ps[:, 6:8, :]
        psA_rows = psA.rearrange("p c (b d) -> p (c b) d", d=D)
        psM_rows = psM.rearrange("p c (b d) -> p (c b) d", d=D)
        psC_rows = psC.rearrange("p c (b d) -> p (c b) d", d=D)
        psA_heads = psA.rearrange("p c (h k) -> p (c h) k", k=P)
        psC_S = ps[:, 6, :].rearrange("p (b k) -> p b k", b=B)
        psC_PT = [ps[:, 6 + l, :].rearrange("p (b k) -> p b k", b=B) for l in range(L)]
        psAV = ps[:, 2, 0:H * VW].rearrange("p (h c) -> p h c", h=H)

        ld_raw = [sem(f"ld_raw{n}") for n in range(4)]
        ld_ln, ld_vec = sem("ld_ln"), sem("ld_vec")
        const_ok = sem("const_ok")
        prep_pe = sem("prep_pe")
        prep_act = sem("prep_act")
        prep_dve = sem("prep_dve")
        ld_x = [sem(f"ld_x{n}") for n in range(2)]
        ld_adjA, ld_adjC = sem("ld_adjA"), sem("ld_adjC")
        st_out = sem("st_out")
        stk = sem("stk")
        STK = 12 * 16
        waited = sem("waited")
        def each_layer(name):
            return [sem(f"{name}{l}") for l in range(L)]

        t_xT, t_S = sem("t_xT"), sem("t_S")
        t_qk, a_qk, d_qk = ([sem(f"{e}_qk{i}") for i in range(4)] for e in "tad")
        t_v, a_v, d_v = ([sem(f"{e}_v{i}") for i in range(2)] for e in "tad")
        t_PT, t_AV, t_oT, t_wo = sem("t_PT"), sem("t_AV"), sem("t_oT"), sem("t_wo")
        t_mT, t_up, t_down = sem("t_mT"), sem("t_up"), sem("t_down")
        t_cT, t_cq, t_ck = each_layer("t_cT"), each_layer("t_cq"), each_layer("t_ck")
        t_cS, t_cW, t_cPT, t_cPV = (each_layer("t_" + n) for n in ("cS", "cW", "cPT", "cPV"))
        a_xT, a_exp = sem("a_xT"), sem("a_exp")
        a_PT, a_oT, a_mT = sem("a_PT"), sem("a_oT"), sem("a_mT")
        a_gelu, a_hi = sem("a_gelu"), sem("a_hi")
        a_cT, a_cq, a_ck, a_cW = (each_layer("a_" + n) for n in ("cT", "cq", "ck", "cW"))
        a_cexp, a_cPT = each_layer("a_cexp"), each_layer("a_cPT")
        d_xT = sem("d_xT")
        d_mt, d_mA, d_mC = sem("d_mt"), sem("d_mA"), sem("d_mC")
        d_S, d_max, d_nb = sem("d_S"), sem("d_max"), sem("d_nb")
        d_PT, d_rec, d_o, d_oT, d_x1 = (sem("d_" + n) for n in ("PT", "rec", "o", "oT", "x1"))
        d_mT, d_lo, d_x2 = (sem("d_" + n) for n in ("mT", "lo", "x2"))
        d_cT, d_cS, d_cmax, d_cnb = (each_layer("d_" + n) for n in ("cT", "cS", "cmax", "cnb"))
        d_crec, d_csc, d_cy = (each_layer("d_" + n) for n in ("crec", "csc", "cy"))
        d_st, d_mv, d_xh = ([sem(f"{n}{k}") for k in range(4)] for n in ("d_st", "d_mv", "d_xh"))
        p_ve, p_rs = ([sem(f"{n}{k}") for k in range(4)] for n in ("p_ve", "p_rs"))
        p_xb, p_x1b, p_cW, p_lo = sem("p_xb"), sem("p_x1b"), sem("p_cW"), sem("p_lo")
        p_cg, p_c = each_layer("p_cg"), each_layer("p_c")

        def need(eng, signal, g, per, k):
            pair, odd = g
            if isinstance(pair, int):
                count = min((2 * pair + odd) * per + k, NG * per)
                if count > 0:
                    eng.wait_ge(signal, count)
            else:
                eng.wait_ge(signal, pair * (2 * per) + (odd * per + k))

        def apart(eng):
            eng.sem_inc(waited, 1)

        def need_apart(eng, signal, g, per, k):
            need(eng, signal, g, per, k)
            apart(eng)

        def mm3(pe, dst, lh, ll, rh, rl, start, stop, **kw):
            pe.matmul(dst, lh, rh, start=start, stop=False, **kw)
            pe.matmul(dst, lh, rl, start=False, stop=False, **kw)
            return pe.matmul(dst, ll, rh, start=False, stop=stop, **kw)

        def split_hidden(eng, g, c, done):
            need(eng, a_hi, g, FC, c + 1)
            eng.tensor_tensor(hid_l[:, c % RING, :], hidden[:, c % 2, :],
                              hid_h[:, c % RING, :].bitcast(F32), ALU.subtract).then_inc(done, 1)

        def steps(order, it, odd):
            for entry in order:
                at = max(entry.rfind("+"), entry.rfind("-"))
                ahead = int(entry[at:])
                par = (odd + ahead) % 2
                pair = it + (odd + ahead - par) // 2
                if not isinstance(it, int) or 0 <= 2 * pair + par < NG:
                    yield (*entry[:at].split("."), (pair, par))

        def run(eng, order, iteration):
            aheads = [int(entry[-2:]) for entry in order]
            start, stop = (4 - min(aheads)) // 2, (NG - max(aheads)) // 2
            for n in range(-max(aheads), 2 * start):
                iteration(n // 2, n % 2)
            with eng.Fori(start, stop) as it:
                iteration(it, 0)
                iteration(it, 1)
            for n in range(2 * stop, NG - min(aheads)):
                iteration(n // 2, n % 2)

        NVEC = 10 + 2 * L
        QSCALE, CSCALE = 1 / math.sqrt(HD), 1 / math.sqrt(P)
        layer_qk = [ps[:, 3 + l, :].rearrange("p (w c f) -> p w c f", w=2, c=KC) for l in range(L)]
        layer_w = [ps[:, 5 + l, :].rearrange("p (c e) -> p c e", c=KC) for l in range(L)]
        halves = []
        for c in range(KC):
            halves += [(wqk_h[:, c, 0:D], wqk_l[:, c, 0:D], raw_qkvo[:, 0, c], ln_q[:, c:c + 1]),
                       (wqk_h[:, c, D:2 * D], wqk_l[:, c, D:2 * D], raw_qkvo[:, 1, c], ln_col[:, 0, c:c + 1]),
                       (wv_h[:, c], wv_l[:, c], raw_qkvo[:, 2, c], ln_col[:, 0, c:c + 1])]
        halves += [(wo_h[:, :, :], wo_l[:, :, :], raw_qkvo[:, 3], 1.0)]
        HALVES_QKVO = len(halves)
        for c in range(KC):
            halves += [(w1_h[:, c], w1_l[:, c], raw_w1[:, c], ln_col[:, 2, c:c + 1])]
        HALVES_W1 = len(halves)
        halves += [(cqk_h[:, 0, :, 0:P], cqk_l[:, 0, :, 0:P], layer_qk[0][:, 0], CSCALE),
                   (cqk_h[:, 0, :, P:2 * P], cqk_l[:, 0, :, P:2 * P], layer_qk[0][:, 1], 1.0),
                   (cw_h[:, 0], cw_l[:, 0], layer_w[0], 1.0)]
        HALVES_C0 = len(halves)
        for c in range(KC):
            gain = cln_col[:, 0, c:c + 1]
            halves += [(cqk_h[:, 1, c, 0:P], cqk_l[:, 1, c, 0:P], layer_qk[1][:, 0, c], cgq[:, c:c + 1]),
                       (cqk_h[:, 1, c, P:2 * P], cqk_l[:, 1, c, P:2 * P], layer_qk[1][:, 1, c], gain),
                       (cw_h[:, 1, c], cw_l[:, 1, c], layer_w[1][:, c], gain)]
        HALVES_L1 = len(halves)
        halves += [(w2_h[:, :, :], w2_l[:, :, :], raw_w2, 1.0)]
        PREP_DVE = 14 + len(halves)
        BV_MADE = 1 + HALVES_W1 + 6
        L1_COPIED = BV_MADE + 3
        block = ctx.enter_context(nc.Block())

        @block.sync
        def _(sp):
            for n, v in enumerate((ln1_g, ln1_b, ln2_g, ln2_b)):
                sp.dma_start(ln_col[:, n, :], v.rearrange("(c p) -> p c", p=P),
                             allow_slow_non_contiguous=True).then_inc(ld_ln, 16)

            def rows(dram, g):
                return dram[bass.ds(g[0], 1), g[1]].rearrange("o p b d -> p (o b) d")

            def weights():
                for n, w in enumerate((wq, wk, wv, wo)):
                    sp.dma_start(raw_qkvo[:, n], w.rearrange("(c p) n -> p c n", p=P)).then_inc(ld_raw[0], 16)
                sp.dma_start(raw_w1, w1.rearrange("(c p) n -> p c n", p=P)).then_inc(ld_raw[1], 16)
                for l in range(L):
                    sp.dma_start(raw_cqk[:, l, 0], cWq[l]).then_inc(ld_raw[3], 16)
                    sp.dma_start(raw_cqk[:, l, 1], cWk[l]).then_inc(ld_raw[3], 16)
                    sp.dma_start(raw_cw[:, l], cWc[l].rearrange("(c p) n -> p c n", p=P)).then_inc(ld_raw[3], 16)
                sp.dma_start(raw_w2, w2.rearrange("(c p) n -> p c n", p=P)).then_inc(ld_raw[2], 16)

            def iteration(it, odd):
                for stage, what, g in steps(SYNC, it, odd):
                    if stage == "N":
                        need_apart(sp, d_x1, g, 1, -1)
                        sp.dma_start(xin[:, g[1]], rows(x_dram, g)).then_inc(ld_x[g[1]], 16)
                    elif what == "stk":
                        need_apart(sp, t_S, g, B, 0)
                        for i in range(4):
                            need_apart(sp, a_qk[i], g, 1, 1)
                            need_apart(sp, d_qk[i], g, 1, 1)
                        for slot, parts in enumerate((slice(0, 3, 2), slice(0, 4, 3), slice(1, 3, 1))):
                            for j in range(4):
                                sp.dma_start(qkS[32 * slot:32 * slot + 32, :, j],
                                             qk16[32 * j:32 * j + 32, parts]).then_inc(stk, 16)
                    elif what == "ldA":
                        need_apart(sp, d_mC, g, 1, -2)
                        need_apart(sp, d_mA, g, 1, 0)
                        sp.dma_start(adj_in[:, :, :], rows(adj_dram, g)).then_inc(ld_adjA, 16)
                    elif what == "ldC":
                        need_apart(sp, d_mA, g, 1, 3)
                        need_apart(sp, d_mC, g, 1, 0)
                        sp.dma_start(adj_in[:, :, :], rows(adj_dram, g)).then_inc(ld_adjC, 16)
                    elif what == "sto":
                        need_apart(sp, p_c[1], g, 1, 1)
                        sp.dma_start(rows(out_dram, g), x3[:, :, :]).then_inc(st_out, 16)

            weights()
            run(sp, SYNC, iteration)
            sp.wait_ge(st_out, 16 * NG)

        @block.gpsimd
        def _(pool):
            pool.memset(ident[:, :], 0.0).then_inc(const_ok, 1)
            pool.memset(minus_half[:, :], -0.5).then_inc(const_ok, 1)
            pool.memset(eps_cols[:, :], EPS).then_inc(const_ok, 1)
            pool.memset(v_h[:, :, :, HD:VW], 1.0).then_inc(const_ok, 1)
            pool.memset(v_l[:, :, :, HD:VW], 0.0).then_inc(const_ok, 1)
            pool.wait_ge(const_ok, 5)
            pool.affine_select(out=ident[:, :], in_=ident[:, :], compare_op=ALU.not_equal, fill=1.0,
                               base=0, pattern=[[-1, P]], channel_multiplier=1).then_inc(const_ok, 1)

            def column(dst, v, pattern="(c p) -> p c"):
                sizes = {"p": P} if "c" in pattern else {}
                pool.dma_start(dst, v.rearrange(pattern, **sizes), allow_slow_non_contiguous=True)\
                    .then_inc(ld_vec, 16)

            column(bqk_col[:, 0:2], bq)
            column(bqk_col[:, 2:4], bk)
            column(bv_col[:, :], bv)
            column(b1_col[:, :], b1)
            column(cb_col[:, 0, :], cbq, "l p -> p l")
            column(cb_col[:, 1, :], cbk, "l p -> p l")
            column(cln_col[:, 0, :], c_g[0])
            column(cln_col[:, 1, :], c_b[0])
            pool.dma_start(bo_row[:, :], bo.partition_broadcast(P)).then_inc(ld_vec, 16)
            pool.dma_start(b2_row[:, :], b2.partition_broadcast(P)).then_inc(ld_vec, 16)
            for l in range(L):
                pool.dma_start(cg_row[:, l, :], c_g[l].partition_broadcast(P)).then_inc(ld_vec, 16)
                pool.dma_start(cb_row[:, l, :], c_b[l].partition_broadcast(P)).then_inc(ld_vec, 16)
            pool.wait_ge(const_ok, 6)

            def rsqrt(g, n):
                need(pool, d_mv[n], g, 1, 1)
                pool.tensor_tensor(ve[:, n], mv[:, n, :, 1], eps_cols[:, :], ALU.add).then_inc(p_ve[n], 1)
                need(pool, p_ve[n], g, 1, 1)
                pool.tensor_tensor(rs[:, n], ve[:, n], minus_half[:, :], ALU.pow).then_inc(p_rs[n], 1)

            def over_graphs(row):
                return row.unsqueeze(1).broadcast_to([P, B, D])

            def affine(g, l, dst, src):
                need(pool, d_xh[2 + l], g, 1, 1)
                pool.tensor_tensor(dst, src, over_graphs(cg_row[:, l, :]), ALU.mult).then_inc(p_cg[l], 1)
                need(pool, p_cg[l], g, 1, 1)
                pool.tensor_tensor(dst, dst, over_graphs(cb_row[:, l, :]), ALU.add).then_inc(p_c[l], 1)

            NORMS = {"N": 0, "A": 1, "C0": 2, "C1": 3}

            def iteration(it, odd):
                for stage, what, g in steps(GPSIMD, it, odd):
                    if what == "rs":
                        rsqrt(g, NORMS[stage])
                    elif what == "cWb":
                        need(pool, a_cW[1], g, 1, 1)
                        pool.tensor_tensor(cW, cW, over_graphs(cwb_row[:, :]), ALU.add)\
                            .then_inc(p_cW, 1)
                    elif stage == "C0" and what == "af":
                        need(pool, st_out, g, 16, 0)
                        affine(g, 0, x3[:, :, :], xh3[:, :, :])
                    elif stage == "C1" and what == "af":
                        affine(g, 1, x3[:, :, :], x3[:, :, :])
                    elif what == "x1b":
                        need(pool, d_xh[1], g, 1, 1)
                        pool.tensor_tensor(x1, x1, over_graphs(b2_row[:, :]), ALU.add).then_inc(p_x1b, 1)
                    elif what == "xb":
                        need(pool, d_xh[0], g, 1, 1)
                        pool.tensor_tensor(xin[:, g[1]], xin[:, g[1]], over_graphs(bo_row[:, :]),
                                           ALU.add).then_inc(p_xb, 1)
                    elif what[:2] == "lo":
                        split_hidden(pool, g, int(what[2]), p_lo)

            pool.wait_ge(prep_dve, PREP_DVE)
            run(pool, GPSIMD, iteration)

        @block.scalar
        def _(act):
            act.wait_ge(prep_dve, 1)
            act.wait_ge(ld_raw[0], 16 * 4)
            for n, (hi, _, raw, gain) in enumerate(halves):
                if n == HALVES_QKVO:
                    act.wait_ge(ld_raw[1], 16)
                if n == HALVES_W1:
                    act.wait_ge(prep_pe, 3)
                if n == HALVES_C0:
                    act.wait_ge(prep_dve, L1_COPIED)
                if n == HALVES_L1:
                    act.wait_ge(ld_raw[2], 16)
                act.activation(hi, raw, ACT.Copy, scale=gain).then_inc(prep_act, 1)
            act.wait_ge(prep_dve, PREP_DVE)
            act.wait_ge(const_ok, 6)

            def iteration(it, odd):
                for stage, what, g in steps(SCALAR, it, odd):
                    b = int(what[-1]) if what[-1].isdigit() else None
                    if stage == "N":
                        need(act, t_xT, g, 1, 1)
                        for used in (*t_qk, *t_v):
                            need(act, used, g, 1, 0)
                        act.copy(xT_h[:, :, :], psC).then_inc(a_xT, 1)
                    elif what in QK:
                        i = QK.index(what)
                        need(act, t_qk[i], g, 1, 1)
                        need(act, stk, g, STK, 0)
                        act.activation(qk16[:, 2 * (i // 2), i % 2, :], psQ[i % 2], ACT.Identity,
                                       bias=bqk_col[:, i:i + 1]).then_inc(a_qk[i], 1)
                    elif stage == "Q":
                        need(act, t_v[b], g, 1, 1)
                        need(act, t_AV, g, B, 0)
                        act.copy(v_h[:, 2 * b:2 * b + 2, :, 0:HD].rearrange("p b h d -> p (b h) d"),
                                 psQ[b].rearrange("p (n d) -> p n d", d=HD)).then_inc(a_v[b], 1)
                    elif what[:3] == "exp":
                        need(act, d_nb, g, B, b + 1)
                        for h in range(H):
                            last = act.activation(sc[:, b % 2, h], sc[:, b % 2, h], ACT.Exp,
                                                  bias=nbias[:, b, h:h + 1])
                        last.then_inc(a_exp, 1)
                    elif what[:2] == "PT" and stage == "A":
                        need(act, t_PT, g, B, b + 1)
                        need(act, t_AV, g, B, b - 1)
                        act.copy(pT16[:, b % 2, 0], psA_heads).then_inc(a_PT, 1)
                    elif what == "oT":
                        need(act, t_oT, g, 1, 1)
                        need(act, t_up, g, FC, 0)
                        act.copy(rot_h[:, :, :], psA).then_inc(a_oT, 1)
                    elif what == "mT":
                        need(act, t_mT, g, 1, 1)
                        act.copy(rot_h[:, :, :], psM).then_inc(a_mT, 1)
                    elif what[:2] == "up":
                        need(act, t_up, g, FC, b + 1)
                        need(act, t_down, g, FC, b + 1 - RING)
                        need(act, (d_lo, p_lo)[b % 2], g, FC // 2, b // 2)
                        act.activation(hidden[:, b % 2, :], psUp, ACT.Gelu,
                                       bias=b1_col[:, b:b + 1]).then_inc(a_gelu, 1)
                        need(act, a_gelu, g, FC, b + 1)
                        act.copy(hid_h[:, b % RING, :], hidden[:, b % 2, :]).then_inc(a_hi, 1)
                    else:
                        l = int(stage[1])
                        if what == "xT":
                            need(act, t_cT[l], g, 1, 1)
                            need(act, t_cW[1 - l], g, 1, -1 if l == 0 else 2)
                            act.copy(cT_h[:, :, :], psC).then_inc(a_cT[l], 1)
                        elif what in ("q", "k"):
                            i = "qk".index(what)
                            need(act, (t_cq, t_ck)[i][l], g, 1, 1)
                            need(act, t_cS[1 - l], g, 1, -1 if l == 0 else 2)
                            act.activation((cq, ck)[i][:, :], psC[:, i, :], ACT.Identity,
                                           bias=cb_col[:, i, l:l + 1]).then_inc((a_cq, a_ck)[i][l], 1)
                        elif what == "ex":
                            need(act, d_cnb[l], g, 1, 1)
                            for b in range(B):
                                last = act.activation(cs[:, l, b], cs[:, l, b], ACT.Exp,
                                                      bias=cmax[:, l, b:b + 1],
                                                      accum_out=csum[:, l, b:b + 1])
                            last.then_inc(a_cexp[l], 1)
                        elif what == "xW":
                            need(act, t_cW[l], g, 1, 1)
                            need(act, t_cPV[1 - l], g, 1, -1 if l == 0 else 2)
                            act.copy(cW, psC_rows).then_inc(a_cW[l], 1)
                        elif what == "PT":
                            need(act, t_cPT[l], g, 1, 1)
                            act.copy(cs[:, l], psC_PT[l]).then_inc(a_cPT[l], 1)

            run(act, SCALAR, iteration)

        @block.vector
        def _(dve):
            made = [0]

            def prep(instruction):
                made[0] += 1
                instruction.then_inc(prep_dve, 1)

            def prepped():
                dve.wait_ge(prep_dve, made[0])

            def lows(start, stop):
                for n in range(start, stop):
                    hi, lo, raw, gain = halves[n]
                    made = n + 1
                    for layer_from, layer_to in ((HALVES_W1, HALVES_C0), (HALVES_C0, HALVES_L1)):
                        if layer_from <= n < layer_to:
                            made = layer_to
                    dve.wait_ge(prep_act, made)
                    prep(dve.scalar_tensor_tensor(lo, raw, gain, hi.bitcast(F32), ALU.mult, ALU.subtract))

            def stats(g, n, rows):
                for b in range(B):
                    last = dve.bn_stats(st[:, n, b, :], rows[:, b, :])
                last.then_inc(d_st[n], 1)
                need(dve, d_st[n], g, 1, 1)
                apart(dve)
                for b in range(B):
                    last = dve.bn_aggr(mv[:, n, b, :], st[:, n, b, :])
                last.then_inc(d_mv[n], 1)

            def norm(g, n, dst, src):
                need(dve, d_mv[n], g, 1, 1)
                need(dve, p_rs[n], g, 1, 1)
                for b in range(B):
                    last = dve.tensor_scalar(dst[:, b], src[:, b], mv[:, n, b, 0:1], rs[:, n, b:b + 1],
                                             ALU.subtract, ALU.mult)
                last.then_inc(d_xh[n], 1)

            dve.wait_ge(ld_ln, 16 * 4)
            prep(dve.tensor_scalar(ln_q[:, :], ln_col[:, 0, :], QSCALE, None, ALU.mult))
            lows(0, HALVES_W1)
            dve.wait_ge(ld_vec, 16 * NVEC)
            prep(dve.tensor_copy(cb_rep, cln_col[:, 1, :].unsqueeze(2).broadcast_to([P, KC, P])))
            prep(dve.tensor_scalar(cgq[:, :], cln_col[:, 0, :], CSCALE, None, ALU.mult))
            dve.wait_ge(prep_pe, 1)
            prep(dve.tensor_tensor(bqk_col[:, :], bqk_col[:, :], ps[:, 0, 0:4], ALU.add))
            prep(dve.tensor_tensor(bv_col[:, :], bv_col[:, :], ps[:, 0, 4:6], ALU.add))
            prepped()
            prep(dve.tensor_scalar(bqk_col[:, 0:2], bqk_col[:, 0:2], QSCALE, None, ALU.mult))
            prep(dve.tensor_copy(bv_rep, bv_col[:, :].unsqueeze(2).broadcast_to([P, KC, P])))
            assert made[0] == BV_MADE
            dve.wait_ge(prep_pe, 2)
            prep(dve.tensor_tensor(b1_col[:, :], b1_col[:, :], ps[:, 2, 0:FC], ALU.add))
            dve.wait_ge(prep_pe, 3)
            prep(dve.tensor_copy(cqkT, layer_qk[1]))
            prep(dve.tensor_copy(cwT, layer_w[1]))
            assert made[0] == L1_COPIED
            lows(HALVES_W1, HALVES_L1)
            dve.wait_ge(prep_pe, 4)
            prep(dve.tensor_tensor(bo_row[:, :], bo_row[:, :], ps[:, 1, 0:D], ALU.add))
            dve.wait_ge(prep_pe, 5)
            prep(dve.tensor_tensor(cb_col[:, :, 1], cb_col[:, :, 1], ps[:, 0, 0:2], ALU.add))
            prep(dve.tensor_copy(cwb_row[:, :], ps[:, 7, 0:D]))
            prepped()
            prep(dve.tensor_scalar(cb_col[:, 0, :], cb_col[:, 0, :], CSCALE, None, ALU.mult))
            lows(HALVES_L1, len(halves))
            assert made[0] == PREP_DVE, made[0]
            prepped()
            dve.wait_ge(const_ok, 6)

            def iteration(it, odd):
                for stage, what, g in steps(VECTOR, it, odd):
                    b = int(what[-1]) if what[-1].isdigit() else None
                    if what == "mA":
                        need(dve, ld_adjA, g, 16, 16)
                        need(dve, d_S, g, B, 0)
                        adj_f = adj_in[:, :, :].bitcast(F32)
                        dve.tensor_scalar(biasA[:, :, :], adj_in[:, :, :], 0, -1.0, ALU.is_gt, ALU.add)\
                           .then_inc(d_mt, 1)
                        need(dve, d_mt, g, 2, 1)
                        dve.scalar_tensor_tensor(adj_f, adj_in[:, :, :], 0.1, adj_in[:, :, :],
                                                 ALU.mult, ALU.mult).then_inc(d_mt, 1)
                        need(dve, d_mt, g, 2, 2)
                        dve.scalar_tensor_tensor(biasA[:, :, :], biasA[:, :, :], -MASKED, adj_f,
                                                 ALU.mult, ALU.add).then_inc(d_mA, 1)
                    elif what == "mC":
                        need(dve, ld_adjC, g, 16, 16)
                        need(dve, d_cS[1], g, 1, -1)
                        dve.tensor_scalar(biasC[:, g[1]], adj_in[:, :, :], 0, MASKED, ALU.is_equal, ALU.mult)\
                           .then_inc(d_mC, 1)
                    elif stage == "N" and what == "st":
                        need(dve, ld_x[g[1]], (g[0], 0), 8, 16)
                        stats(g, 0, xin[:, g[1]])
                    elif stage == "N" and what == "xh":
                        need(dve, t_xT, g, 1, 0)
                        norm(g, 0, xhatN, xin[:, g[1]])
                    elif stage == "N":
                        need(dve, a_xT, g, 1, 1)
                        dve.tensor_tensor(xT_l[:, :, :], psC, xT_h[:, :, :].bitcast(F32), ALU.subtract)\
                           .then_inc(d_xT, 1)
                    elif what in QK:
                        i = QK.index(what)
                        need(dve, a_qk[i], g, 1, 1)
                        dve.scalar_tensor_tensor(qk16[:, 2 * (i // 2) + 1, i % 2, :], psQ[i % 2],
                                                 bqk_col[:, i:i + 1], qk16[:, 2 * (i // 2), i % 2, :],
                                                 ALU.add, ALU.subtract).then_inc(d_qk[i], 1)
                    elif stage == "Q":
                        need(dve, a_v[b], g, 1, 1)
                        dve.tensor_tensor(
                            v_l[:, 2 * b:2 * b + 2, :, 0:HD].rearrange("p b h d -> p (b h) d"),
                            psQ[b].rearrange("p (n d) -> p n d", d=HD),
                            v_h[:, 2 * b:2 * b + 2, :, 0:HD].rearrange("p b h d -> p (b h) d"),
                            ALU.subtract).then_inc(d_v[b], 1)
                    elif stage == "A" and what[:1] == "S":
                        need(dve, t_S, g, B, b + 1)
                        need(dve, d_mA, g, 1, 1)
                        need(dve, t_PT, g, B, b - 1)
                        dve.tensor_tensor(sc[:, b % 2], psA_heads,
                                          biasA[:, b].unsqueeze(1).broadcast_to([P, H, P]),
                                          ALU.add).then_inc(d_S, 1)
                    elif stage == "A" and what[:3] == "max":
                        need(dve, d_S, g, B, b + 1)
                        dve.tensor_reduce(nmax[:, b, :], sc[:, b % 2], AX.X, ALU.max).then_inc(d_max, 1)
                        need(dve, d_max, g, B, b + 1)
                        dve.tensor_scalar(nbias[:, b, :], nmax[:, b, :], -1.0, P_SCALE,
                                          ALU.mult, ALU.add).then_inc(d_nb, 1)
                    elif stage == "A" and what[:2] == "PT":
                        need(dve, a_PT, g, B, b + 1)
                        dve.tensor_tensor(pT16[:, b % 2, 1], psA_heads, pT16[:, b % 2, 0], ALU.subtract)\
                           .then_inc(d_PT, 1)
                    elif what[:2] == "AV":
                        need(dve, t_AV, g, B, b + 1)
                        dve.reciprocal(rec[:, b, :], psAV[:, :, HD]).then_inc(d_rec, 1)
                        need(dve, d_rec, g, B, b + 1)
                        if b == 0:
                            need(dve, t_mT, g, 1, 0)
                        dve.tensor_tensor(o_rows[:, b].rearrange("p (h d) -> p h d", h=H),
                                          psAV[:, :, 0:HD],
                                          rec[:, b, :].unsqueeze(2).broadcast_to([P, H, HD]),
                                          ALU.mult).then_inc(d_o, 1)
                    elif what == "oT":
                        need(dve, a_oT, g, 1, 1)
                        dve.tensor_tensor(rot_l[:, :, :], psA, rot_h[:, :, :].bitcast(F32), ALU.subtract)\
                           .then_inc(d_oT, 1)
                    elif what == "wo":
                        need(dve, t_wo, g, 1, 1)
                        need(dve, p_xb, g, 1, 1)
                        need(dve, d_x2, g, 1, 0)
                        dve.tensor_tensor(x1, psA_rows, xin[:, g[1]], ALU.add).then_inc(d_x1, 1)
                    elif stage == "A" and what == "st":
                        need(dve, d_x1, g, 1, 1)
                        stats(g, 1, x1)
                    elif stage == "A" and what == "xh":
                        norm(g, 1, xhat, x1)
                    elif what == "mT":
                        need(dve, a_mT, g, 1, 1)
                        dve.tensor_tensor(rot_l[:, :, :], psM, rot_h[:, :, :].bitcast(F32), ALU.subtract)\
                           .then_inc(d_mT, 1)
                    elif what[:2] == "lo":
                        split_hidden(dve, g, b, d_lo)
                    elif what == "x2":
                        need(dve, t_down, g, FC, FC)
                        need(dve, p_x1b, g, 1, 1)
                        need(dve, d_cy[0], g, 1, 0)
                        dve.tensor_tensor(x2, psM_rows, x1, ALU.add).then_inc(d_x2, 1)
                    else:
                        l = int(stage[1])
                        rows3 = (xh3, x3)[l]
                        if what == "xT":
                            need(dve, a_cT[l], g, 1, 1)
                            dve.tensor_tensor(cT_l[:, :, :], psC, cT_h[:, :, :].bitcast(F32), ALU.subtract)\
                               .then_inc(d_cT[l], 1)
                        elif what == "S":
                            need(dve, t_cS[l], g, 1, 1)
                            need(dve, d_mC, g, 1, 1)
                            need(dve, t_cPV[l], g, 1, 0)
                            dve.tensor_tensor(cs[:, l], psC_S, biasC[:, g[1]], ALU.add).then_inc(d_cS[l], 1)
                        elif what == "max":
                            need(dve, d_cS[l], g, 1, 1)
                            dve.tensor_reduce(cneg[:, l], cs[:, l], AX.X, ALU.max).then_inc(d_cmax[l], 1)
                            need(dve, d_cmax[l], g, 1, 1)
                            dve.tensor_scalar(cmax[:, l], cneg[:, l], -1.0, None, ALU.mult).then_inc(d_cnb[l], 1)
                        elif what == "PV":
                            need(dve, a_cexp[l], g, 1, 1)
                            dve.reciprocal(crec[:, l], csum[:, l]).then_inc(d_crec[l], 1)
                            need(dve, d_crec[l], g, 1, 1)
                            dve.scalar_tensor_tensor(cscale[:, l], cmax[:, l], -MASKED / 10, crec[:, l],
                                                     ALU.is_lt, ALU.mult).then_inc(d_csc[l], 1)
                            need(dve, d_csc[l], g, 1, 1)
                            need(dve, t_cPV[l], g, 1, 1)
                            need(dve, p_c[0], g, 1, l)
                            if l == 0:
                                need(dve, t_cT[1], g, 1, 0)
                            residual = (x2, x3)[l]
                            for b in range(B):
                                last = dve.scalar_tensor_tensor(rows3[:, b], psC_rows[:, b],
                                                                cscale[:, l, b:b + 1], residual[:, b],
                                                                ALU.mult, ALU.add)
                            last.then_inc(d_cy[l], 1)
                        elif what == "st":
                            need(dve, d_cy[l], g, 1, 1)
                            stats(g, 2 + l, rows3)
                        elif what == "xh":
                            norm(g, 2 + l, rows3, rows3)

            run(dve, VECTOR, iteration)

        @block.tensor
        def _(pe):
            pe.wait_ge(const_ok, 6)
            pe.wait_ge(ld_ln, 16 * 4)
            pe.wait_ge(ld_raw[0], 16 * 4)
            for t in range(6):
                for c in range(KC):
                    last = pe.matmul(ps[:, 0, t:t + 1], raw_qkvo[:, t // 2, c, (t % 2) * P:(t % 2) * P + P],
                                     ln_col[:, 1, c:c + 1], start=(c == 0), stop=(c == KC - 1))
            last.then_inc(prep_pe, 1)
            pe.wait_ge(ld_raw[1], 16)
            for t in range(FC):
                for c in range(KC):
                    last = pe.matmul(ps[:, 2, t:t + 1], raw_w1[:, c, t * P:t * P + P],
                                     ln_col[:, 3, c:c + 1], start=(c == 0), stop=(c == KC - 1))
            last.then_inc(prep_pe, 1)
            pe.wait_ge(ld_raw[3], 16 * 3 * L)
            for l in range(L):
                for w in range(2):
                    for c in range(KC):
                        pe.transpose(ps[:, 3 + l, (w * KC + c) * P:(w * KC + c + 1) * P],
                                     raw_cqk[:, l, w, c * P:(c + 1) * P], ident[:, :])
                for c in range(KC):
                    for e in range(KC):
                        last = pe.transpose(ps[:, 5 + l, c * D + e * P:c * D + (e + 1) * P],
                                            raw_cw[:, l, e, c * P:(c + 1) * P], ident[:, :])
            last.then_inc(prep_pe, 1)
            pe.wait_ge(prep_dve, BV_MADE)
            for c in range(KC):
                last = pe.matmul(ps[:, 1, 0:D], bv_rep[:, c], raw_qkvo[:, 3, c],
                                 start=(c == 0), stop=(c == KC - 1))
            last.then_inc(prep_pe, 1)
            pe.wait_ge(prep_dve, L1_COPIED)
            for w in range(2):
                for c in range(KC):
                    pe.matmul(ps[:, 0, w:w + 1], cqkT[:, w, c], cln_col[:, 1, c:c + 1],
                              start=(c == 0), stop=(c == KC - 1))
            for c in range(KC):
                last = pe.matmul(ps[:, 7, 0:D], cb_rep[:, c], cwT[:, c],
                                 start=(c == 0), stop=(c == KC - 1))
            last.then_inc(prep_pe, 1)
            pe.wait_ge(prep_dve, PREP_DVE)

            def transposes(dst, rows, signal):
                for c in range(KC):
                    for b in range(B):
                        last = pe.transpose(dst[:, c, b * P:(b + 1) * P], rows[:, b, c * P:(c + 1) * P],
                                            ident[:, :])
                last.then_inc(signal, 1)

            def to_columns(dst, w_h, w_l, x_h, x_l, n):
                for c in range(KC):
                    last = mm3(pe, dst, w_h[:, c, n:n + P], w_l[:, c, n:n + P], x_h[:, c, :], x_l[:, c, :],
                               start=(c == 0), stop=(c == KC - 1))
                return last

            def to_rows(dst, x_h, x_l, w_h, w_l, b):
                for c in range(KC):
                    last = mm3(pe, dst, x_h[:, c, b * P:(b + 1) * P], x_l[:, c, b * P:(b + 1) * P],
                               w_h[:, c, :], w_l[:, c, :], start=(c == 0), stop=(c == KC - 1))
                return last

            def iteration(it, odd):
                for stage, what, g in steps(TENSOR, it, odd):
                    b = int(what[-1]) if what[-1].isdigit() else None
                    step = stage + "." + what
                    if step == "Q.k0":
                        need(pe, d_v[0], g, 1, 0)
                        if isinstance(it, int):
                            need(pe, d_o, g, B, -4)
                    elif step == "A.S2":
                        need(pe, d_PT, g, B, 1)
                    elif step == "M.up4":
                        need(pe, a_gelu, g, FC, 4)
                        if isinstance(it, int):
                            need(pe, d_v[1], g, 1, 2)
                    elif step == "C0.q":
                        need(pe, d_cT[0], g, 1, 1)
                        if isinstance(it, int):
                            need(pe, d_xT, g, 1, 4)
                            need(pe, d_cy[1], g, 1, -1)
                    elif step == "A.PT1":
                        need(pe, d_S, g, B, 3)
                    elif step == "M.up5":
                        need(pe, a_gelu, g, FC, 5)
                        if isinstance(it, int):
                            need(pe, d_v[1], g, 1, 2)
                    elif step == "C0.k":
                        need(pe, d_cT[0], g, 1, 1)
                        if isinstance(it, int):
                            need(pe, d_xT, g, 1, 4)
                            need(pe, d_cy[1], g, 1, -1)
                    elif step == "Q.q0":
                        need(pe, d_qk[2], g, 1, 1)
                        if isinstance(it, int):
                            need(pe, d_o, g, B, -4)
                    elif step == "M.up6":
                        need(pe, a_gelu, g, FC, 6)
                        if isinstance(it, int):
                            need(pe, d_v[1], g, 1, 2)
                    elif step == "C0.S":
                        need(pe, a_cq[0], g, 1, 1)
                        if isinstance(it, int):
                            need(pe, d_xT, g, 1, 4)
                            need(pe, d_cy[1], g, 1, -1)
                    elif step == "A.S3":
                        need(pe, d_PT, g, B, 2)
                    elif step == "C0.xW":
                        need(pe, d_cS[0], g, 1, 1)
                        need(pe, a_ck[0], g, 1, 1)
                        if isinstance(it, int):
                            need(pe, d_xT, g, 1, 4)
                            need(pe, d_cy[1], g, 1, -1)
                    elif step == "Q.q1":
                        need(pe, a_gelu, g, FC, -9)
                        if isinstance(it, int):
                            need(pe, d_v[1], g, 1, 0)
                    elif step == "A.AV0":
                        need(pe, d_qk[0], g, 1, 2)
                        if isinstance(it, int):
                            need(pe, d_o, g, B, 0)
                    elif step == "A.PT2":
                        need(pe, d_S, g, B, 4)
                    elif step == "A.AV1":
                        need(pe, d_o, g, B, 1)
                        if isinstance(it, int):
                            need(pe, d_qk[0], g, 1, 2)
                    elif step == "Q.k1":
                        need(pe, d_qk[1], g, 1, 1)
                        if isinstance(it, int):
                            need(pe, a_gelu, g, FC, -9)
                    elif step == "C0.PT":
                        need(pe, a_cW[0], g, 1, 1)
                        if isinstance(it, int):
                            need(pe, d_xT, g, 1, 4)
                            need(pe, d_cy[1], g, 1, -1)
                    elif step == "A.PT3":
                        need(pe, d_PT, g, B, 3)
                    elif step == "A.AV2":
                        need(pe, d_o, g, B, 2)
                        if isinstance(it, int):
                            need(pe, d_qk[0], g, 1, 2)
                    elif step == "C1.xT":
                        need(pe, a_cPT[0], g, 1, 2)
                        need(pe, a_cW[0], g, 1, 2)
                        if isinstance(it, int):
                            need(pe, d_xT, g, 1, 5)
                            need(pe, d_cy[1], g, 1, 0)
                    elif step == "M.up7":
                        need(pe, d_qk[3], g, 1, 3)
                        if isinstance(it, int):
                            need(pe, a_gelu, g, FC, 7)
                    elif step == "A.AV3":
                        need(pe, d_o, g, B, 3)
                        if isinstance(it, int):
                            need(pe, d_qk[0], g, 1, 2)
                    elif step == "A.oT":
                        need(pe, d_PT, g, B, 4)
                    elif step == "C0.PV":
                        need(pe, d_cT[1], g, 1, 0)
                        if isinstance(it, int):
                            need(pe, a_cPT[0], g, 1, 1)
                            need(pe, d_xT, g, 1, 4)
                            need(pe, a_cW[0], g, 1, 1)
                    elif step == "A.wo":
                        need(pe, d_oT, g, 1, 1)
                    elif step == "C1.q":
                        need(pe, d_cy[0], g, 1, 2)
                        if isinstance(it, int):
                            need(pe, d_cT[1], g, 1, 1)
                            need(pe, d_xT, g, 1, 5)
                    elif step == "C1.k":
                        need(pe, d_cy[0], g, 1, 2)
                        if isinstance(it, int):
                            need(pe, d_cT[1], g, 1, 1)
                            need(pe, d_xT, g, 1, 5)
                    elif step == "A.S0":
                        need(pe, d_x1, g, 1, 0)
                    elif step == "C1.S":
                        need(pe, a_cq[1], g, 1, 1)
                        if isinstance(it, int):
                            need(pe, d_cy[0], g, 1, 2)
                            need(pe, d_xT, g, 1, 5)
                    elif step == "Q.v1":
                        need(pe, a_gelu, g, FC, -8)
                        if isinstance(it, int):
                            need(pe, d_qk[3], g, 1, 1)
                    elif step == "C1.xW":
                        need(pe, d_cS[1], g, 1, 1)
                        need(pe, a_ck[1], g, 1, 1)
                        if isinstance(it, int):
                            need(pe, d_cy[0], g, 1, 2)
                            need(pe, d_xT, g, 1, 5)
                    elif step == "M.mT":
                        need(pe, d_x2, g, 1, 0)
                    elif step == "A.S1":
                        need(pe, d_S, g, B, 1)
                    elif step == "C1.PT":
                        need(pe, a_cW[1], g, 1, 1)
                        if isinstance(it, int):
                            need(pe, d_cy[0], g, 1, 2)
                            need(pe, d_xT, g, 1, 5)
                    elif step == "Q.v0":
                        need(pe, d_o, g, B, 0)
                        if isinstance(it, int):
                            need(pe, d_qk[0], g, 1, 1)
                    elif step == "M.up0":
                        need(pe, d_v[1], g, 1, 2)
                        if isinstance(it, int):
                            need(pe, a_gelu, g, FC, 0)
                    elif step == "C1.PV":
                        need(pe, a_cW[1], g, 1, 1)
                        need(pe, a_cPT[1], g, 1, 1)
                        if isinstance(it, int):
                            need(pe, d_cy[0], g, 1, 2)
                            need(pe, d_xT, g, 1, 5)
                    elif step == "A.PT0":
                        need(pe, d_S, g, B, 2)
                    elif step == "M.up1":
                        need(pe, a_gelu, g, FC, 1)
                        if isinstance(it, int):
                            need(pe, d_v[1], g, 1, 2)
                    elif step == "N.xT":
                        need(pe, d_cy[1], g, 1, -4)
                        if isinstance(it, int):
                            need(pe, d_cy[0], g, 1, -3)
                            need(pe, d_xT, g, 1, 0)
                    elif step == "M.down0":
                        need(pe, d_mT, g, 1, 1)
                    elif step == "M.up2":
                        need(pe, a_gelu, g, FC, 2)
                        if isinstance(it, int):
                            need(pe, d_v[1], g, 1, 2)
                    elif step == "C0.xT":
                        need(pe, d_xT, g, 1, 4)
                        if isinstance(it, int):
                            need(pe, d_cy[1], g, 1, -1)
                            need(pe, d_cy[0], g, 1, 0)
                    elif step == "M.up3":
                        need(pe, a_gelu, g, FC, 3)
                        if isinstance(it, int):
                            need(pe, d_v[1], g, 1, 2)
                    if stage == "N":
                        need(pe, d_xh[0], g, 1, 1)
                        transposes(psC, xhatN, t_xT)
                    elif what in QK:
                        i = QK.index(what)
                        need(pe, a_xT, g, 1, 1)
                        need(pe, d_xT, g, 1, 1)
                        to_columns(psQ[i % 2], wqk_h, wqk_l, xT_h, xT_l, i * P).then_inc(t_qk[i], 1)
                    elif stage == "Q":
                        need(pe, d_xT, g, 1, 1)
                        for n in range(2):
                            last = to_rows(psQ[b][:, n * D:(n + 1) * D], xT_h, xT_l, wv_h, wv_l, 2 * b + n)
                        last.then_inc(t_v[b], 1)
                    elif stage == "A" and what[:1] == "S":
                        need(pe, stk, g, STK, STK)
                        for h in range(H):
                            last = pe.matmul(psA_heads[:, h], qkS[0:96, 0, h % 4, h // 4, b * P:(b + 1) * P],
                                             qkS[0:96, 1, h % 4, h // 4, b * P:(b + 1) * P],
                                             start=True, stop=True)
                        last.then_inc(t_S, 1)
                    elif stage == "A" and what[:2] == "PT":
                        need(pe, a_exp, g, B, b + 1)
                        for h in range(H):
                            last = pe.transpose(psA_heads[:, h], sc[:, b % 2, h], ident[:, :])
                        last.then_inc(t_PT, 1)
                    elif what[:2] == "AV":
                        need(pe, d_PT, g, B, b + 1)
                        if b == 0:
                            for made in d_v:
                                need(pe, made, g, 1, 1)
                        for h in range(H):
                            last = mm3(pe, psAV[:, h, 0:HD + 1], pT16[:, b % 2, 0, h], pT16[:, b % 2, 1, h],
                                       v_h[:, b, h, 0:HD + 1], v_l[:, b, h, 0:HD + 1],
                                       start=True, stop=True)
                        last.then_inc(t_AV, 1)
                    elif what == "oT":
                        need(pe, d_o, g, B, B)
                        transposes(psA, o_rows, t_oT)
                    elif what == "wo":
                        need(pe, d_oT, g, 1, 1)
                        for b in range(B):
                            last = to_rows(psA_rows[:, b], rot_h, rot_l, wo_h, wo_l, b)
                        last.then_inc(t_wo, 1)
                    elif what == "mT":
                        need(pe, d_xh[1], g, 1, 1)
                        transposes(psM, xhat, t_mT)
                    elif what[:2] == "up":
                        need(pe, d_mT, g, 1, 1)
                        to_columns(psUp, w1_h, w1_l, rot_h, rot_l, b * P).then_inc(t_up, 1)
                    elif what[:4] == "down":
                        c = b
                        need(pe, (d_lo, p_lo)[c % 2], g, FC // 2, c // 2 + 1)
                        for b in range(B):
                            last = mm3(pe, psM_rows[:, b], hid_h[:, c % RING, b * P:(b + 1) * P],
                                       hid_l[:, c % RING, b * P:(b + 1) * P], w2_h[:, c, :], w2_l[:, c, :],
                                       start=(c == 0 and b % 2 == 0), stop=(c == FC - 1),
                                       skip_group_check=True)
                        last.then_inc(t_down, 1)
                    else:
                        l = int(stage[1])
                        if what == "xT":
                            if l == 0:
                                need(pe, d_x2, g, 1, 1)
                            else:
                                need(pe, d_xh[2], g, 1, 1)
                            transposes(psC, (x2, xh3)[l], t_cT[l])
                        elif what in ("q", "k"):
                            i = "qk".index(what)
                            need(pe, d_cT[l], g, 1, 1)
                            to_columns(psC[:, i, :], cqk_h[:, l], cqk_l[:, l], cT_h, cT_l, i * P)\
                                .then_inc((t_cq, t_ck)[i][l], 1)
                        elif what == "S":
                            need(pe, a_cq[l], g, 1, 1)
                            need(pe, a_ck[l], g, 1, 1)
                            for b in range(B):
                                last = pe.matmul(psC_S[:, b], cq[:, b * P:(b + 1) * P], ck[:, b * P:(b + 1) * P],
                                                 start=True, stop=True)
                            last.then_inc(t_cS[l], 1)
                        elif what == "xW":
                            need(pe, d_cT[l], g, 1, 1)
                            for b in range(B):
                                last = to_rows(psC_rows[:, b], cT_h, cT_l, cw_h[:, l], cw_l[:, l], b)
                            last.then_inc(t_cW[l], 1)
                        elif what == "PT":
                            need(pe, a_cexp[l], g, 1, 1)
                            for b in range(B):
                                last = pe.transpose(psC_PT[l][:, b], cs[:, l, b], ident[:, :])
                            last.then_inc(t_cPT[l], 1)
                        elif what == "PV":
                            need(pe, a_cPT[l], g, 1, 1)
                            if l == 0:
                                need(pe, a_cW[0], g, 1, 1)
                            else:
                                need(pe, p_cW, g, 1, 1)
                            for b in range(B):
                                last = pe.matmul(psC_rows[:, b], cs[:, l, b], cW[:, b], start=True, stop=True)
                            last.then_inc(t_cPV[l], 1)

            run(pe, TENSOR, iteration)


_INS = ["x", "adj", "L0_gnn_ln1_g", "L0_gnn_ln1_b", "L0_gnn_ln2_g", "L0_gnn_ln2_b", "L0_gnn_wq",
        "L0_gnn_bq", "L0_gnn_wk", "L0_gnn_bk", "L0_gnn_wv", "L0_gnn_bv", "L0_gnn_wo", "L0_gnn_bo",
        "L0_gnn_w1", "L0_gnn_b1", "L0_gnn_w2", "L0_gnn_b2", "L1_gnn_Wq", "L1_gnn_bq", "L1_gnn_bk",
        "L1_gnn_Wk", "L1_gnn_Wc", "L1_gnn_ln_g", "L1_gnn_ln_b"]


def kernel(**inputs):
    import numpy as _np
    import concourse.bacc as _bacc
    from concourse.bass_utils import run_bass_kernel_spmd as _run

    nc = _bacc.Bacc("TRN2", target_bir_lowering=False, num_devices=1)
    arrays, args = {}, []
    for name in _INS:
        a = _np.ascontiguousarray(inputs[name])
        arrays[f"in_{name}"] = a
        args.append(nc.dram_tensor(f"in_{name}", a.shape, mybir.dt.from_np(a.dtype), kind="ExternalInput").ap())
    args.append(nc.dram_tensor("out_0", inputs["x"].shape, F32, kind="ExternalOutput").ap())
    graph_blocks(nc, *args)
    r = _run(nc, [arrays], core_ids=[0])
    return r.results[0]["out_0"]
```
